# Optimizing a Trainium2 kernel written in Bass

```python
import numpy as np
import jax
import jax.numpy as jnp

def _softmax(x, axis=-1):
    return jax.nn.softmax(x, axis=axis)

def _gelu(x):
    return jax.nn.gelu(x, approximate=True)

def _silu(x):
    return jax.nn.silu(x)

def _sigmoid(x):
    return jax.nn.sigmoid(x)

def _layernorm(x, axis=-1, eps=1e-05):
    m = jnp.mean(x, axis=axis, keepdims=True)
    v = jnp.var(x, axis=axis, keepdims=True)
    return (x - m) / jnp.sqrt(v + eps)

def _scatter_add(tgt, idx, src, axis=0):
    return tgt.at[idx].add(src)

def _segment_sum(src, seg, n):
    return jax.ops.segment_sum(src, seg, n)
kernel_name = 'mk_adaln_ffn_d1_seqx_r4_6548fc'

def setup_inputs(seed: int=0):
    np.random.seed(seed)
    _w = jnp.asarray

    def _rec_inputs():
        import jax
        import jax.numpy as jnp
        _rk = jax.random.key(seed)
        x = -0.000125 + 0.9999 * jax.random.normal(jax.random.fold_in(_rk, 1), (2, 1024, 256), jnp.float32)
        _lenS = 1024 - jax.random.randint(jax.random.fold_in(_rk, 7), (2,), 0, max(1, 1024 // 4) + 1, jnp.int32)
        _lenS2 = 1024 - jax.random.randint(jax.random.fold_in(_rk, 8), (2,), 0, max(1, 1024 // 4) + 1, jnp.int32)
        cond_512 = 0.00782532 + 1.00527 * jax.random.normal(jax.random.fold_in(_rk, 11), (2, 128), jnp.float32)
        return (x, cond_512)
    x, cond_512 = _rec_inputs()

    def _L0_cond_setup():
        import jax, jax.numpy as jnp
        import numpy as np
        IN_DIM = 256
        OUT_DIM = 256
        MU_DIM = 128
        K = 30
        key = jax.random.key(seed)
        k1, k2, k3, k4, k5 = jax.random.split(key, 5)
        B, S = (16, 512)
        x = jax.random.normal(k1, (B, S, IN_DIM), dtype=jnp.float32)
        mu = jax.random.normal(k2, (B, MU_DIM), dtype=jnp.float32)
        W_dec = jax.random.normal(k3, (MU_DIM, (IN_DIM + 1) * K), dtype=jnp.float32) / np.sqrt(MU_DIM)
        b_dec = jax.random.normal(k4, ((IN_DIM + 1) * K,), dtype=jnp.float32) * 0.01
        V = jax.random.normal(k5, (K, OUT_DIM), dtype=jnp.float32) / np.sqrt(K)
        return {'x': x, 'mu': mu, 'W_dec': W_dec, 'b_dec': b_dec, 'V': V}
    _L0_cond_all = _L0_cond_setup()
    _L0_cond_in = {k: v for k, v in _L0_cond_all.items() if k in ('W_dec', 'b_dec', 'V')}
    del _L0_cond_all

    def _L0_ffn_setup():
        import jax, jax.numpy as jnp
        import numpy as np
        E = 8
        K = 2
        D = 256
        H = 256
        B, T = (2, 256)
        key = jax.random.key(seed)
        ks = jax.random.split(key, 6)
        s = 0.02
        return {'x': jax.random.normal(ks[0], (B, T, D), dtype=jnp.float32), 'gate_w': jax.random.normal(ks[1], (E, D), dtype=jnp.float32) * s, 'lb_bias': jnp.zeros((E,), dtype=jnp.float32), 'w1': jax.random.normal(ks[2], (E, H, D), dtype=jnp.float32) * s, 'w2': jax.random.normal(ks[3], (E, D, H), dtype=jnp.float32) * s, 'cfc': jax.random.normal(ks[4], (H, D), dtype=jnp.float32) * s, 'cproj': jax.random.normal(ks[5], (D, H), dtype=jnp.float32) * s}
    _L0_ffn_all = _L0_ffn_setup()
    _L0_ffn_in = {k: v for k, v in _L0_ffn_all.items() if k in ('gate_w', 'lb_bias', 'w1', 'w2', 'cfc', 'cproj')}
    del _L0_ffn_all
    return {'x': x, 'cond_512': cond_512, 'L0_cond_W_dec': _L0_cond_in['W_dec'], 'L0_cond_b_dec': _L0_cond_in['b_dec'], 'L0_cond_V': _L0_cond_in['V'], 'L0_ffn_gate_w': _L0_ffn_in['gate_w'], 'L0_ffn_lb_bias': _L0_ffn_in['lb_bias'], 'L0_ffn_w1': _L0_ffn_in['w1'], 'L0_ffn_w2': _L0_ffn_in['w2'], 'L0_ffn_cfc': _L0_ffn_in['cfc'], 'L0_ffn_cproj': _L0_ffn_in['cproj']}

def reference(x, cond_512, L0_cond_W_dec, L0_cond_b_dec, L0_cond_V, L0_ffn_gate_w, L0_ffn_lb_bias, L0_ffn_w1, L0_ffn_w2, L0_ffn_cfc, L0_ffn_cproj):
    import jax
    import jax.numpy as jnp

    def _L0_cond_ref(x, mu, W_dec, b_dec, V):
        import jax, jax.numpy as jnp
        import numpy as np
        IN_DIM = 256
        OUT_DIM = 256
        MU_DIM = 128
        K = 30
        B = mu.shape[0]
        U = (mu @ W_dec + b_dec).reshape(B, IN_DIM + 1, K)
        param = jnp.einsum('bik,kj->bij', U, V)
        weight = param[:, :-1, :]
        bias = param[:, -1, :]
        out = jnp.einsum('bsd,bde->bse', x, weight)
        out = out + bias[:, None, :]
        return out

    def _L0_ffn_ref(x, gate_w, lb_bias, w1, w2, cfc, cproj):
        import jax, jax.numpy as jnp
        import numpy as np
        E = 8
        K = 2
        D = 256
        H = 256
        B, T = (2, 256)
        Bx, Tx, Dx = x.shape
        logits = jnp.einsum('btd,ed->bte', x, gate_w)
        _, idx = jax.lax.top_k(logits + lb_bias, K)
        sel_logits = jnp.take_along_axis(logits, idx, axis=-1)
        w = jax.nn.sigmoid(sel_logits)
        w = w / (jnp.sum(w, axis=-1, keepdims=True) + 1e-06)
        xf = x.reshape(-1, Dx)
        idxf = idx.reshape(-1, K)
        wf = w.reshape(-1, K)
        onehot = jax.nn.one_hot(idxf, E, dtype=wf.dtype)
        we = jnp.einsum('nke,nk->ne', onehot, wf)
        hidden = jnp.square(jax.nn.relu(jnp.einsum('nd,ehd->neh', xf, w1)))
        expert_out = jnp.einsum('neh,edh->ned', hidden, w2)
        moe_out = jnp.einsum('ned,ne->nd', expert_out, we).reshape(Bx, Tx, Dx)
        sh = jnp.square(jax.nn.relu(jnp.einsum('btd,hd->bth', x, cfc)))
        shared = jnp.einsum('bth,dh->btd', sh, cproj)
        return moe_out + shared
    x = x + _L0_ffn_ref(_L0_cond_ref(x, cond_512, L0_cond_W_dec, L0_cond_b_dec, L0_cond_V), L0_ffn_gate_w, L0_ffn_lb_bias, L0_ffn_w1, L0_ffn_w2, L0_ffn_cfc, L0_ffn_cproj)
    return x

_drawn_inputs = setup_inputs


def setup_inputs(seed=0):
    import zlib

    import numpy as np

    out = dict(_drawn_inputs(seed))
    spreads = {'L0_ffn_lb_bias': (0.0, 0.294)}
    factors = {'L0_cond_b_dec': 2.934}
    for name, (base, spread) in spreads.items():
        noise = np.random.default_rng([zlib.crc32(name.encode()), seed]).standard_normal(out[name].shape)
        drawn = base * np.exp(spread * noise) if base else spread * noise
        out[name] = jnp.asarray(drawn.astype(out[name].dtype))
    for name, factor in factors.items():
        out[name] = (out[name] * factor).astype(out[name].dtype)
    return out
```

```python
from contextlib import ExitStack

import concourse.bass as bass
from concourse import mybir

F32 = mybir.dt.float32
F32R = mybir.dt.float32r
F16 = mybir.dt.float16
I32 = mybir.dt.int32
ALU = mybir.AluOpType
ACT = mybir.ActivationFunctionType
X_AXIS = mybir.AxisListType.X

P = 128
BATCH, SEQ, D = 2, 1024, 256
N = BATCH * SEQ
E, H = 8, 256
MU, RANK = 128, 30
KD = D // P
CH = 512
NC = N // CH
CT = CH // P
G = 2
GN = N // G
GJ = GN // P
GC = NC // G
GT = (2 * GN + E * (P - 1)) // P
NT = G * GT
NQ = NT // 2
RING = 3
WCH = 6
WK = RANK // WCH
STAGE = 4
EW = KD * H + KD * D
BIG = 3.0e38

_WIDTHS = [("mu", BATCH), ("b_main", KD * RANK), ("gate", KD * E), ("lb", E), ("rank_score", E),
           ("token", GJ), ("tile_no", GT), ("b_last", 1), ("ident", P), ("V", D)]
COL, _at = {}, 0
for _name, _width in _WIDTHS:
    COL[_name] = (_at, _at + _width)
    _at += _width
PACK = _at
F16_TRI, F16_ONES, F16_IOTA, F16_TILE, F16_PACK = 0, P, 2 * P, 3 * P, 3 * P + GT + GT % 2


def build_moe(nc, small, small16, wdec, xT, xrows, experts, out):
    rows_dram = [nc.dram_tensor(f"cond_rows{g}", (GN, D), F32, kind="Internal").ap() for g in range(G)]
    y_dram = [nc.dram_tensor(f"expert_rows{g}", ((GT + 1) * P, D), F32, kind="Internal").ap() for g in range(G)]
    rows_v = [a.rearrange("(n t p) d -> n p t d", t=2, p=P) for a in rows_dram]
    y_v = [a.rearrange("(n t p) d -> n p t d", t=2, p=P) for a in y_dram]
    xrows_v = xrows.rearrange("(j p) d -> p j d", p=P)

    with ExitStack() as ctx:
        def sb(name, shape, dt=F32):
            return ctx.enter_context(nc.sbuf_tensor(name, shape, dt))

        def sem(name):
            return ctx.enter_context(nc.semaphore(name))

        pack = sb("pack", [P, PACK])
        pack16 = sb("pack16", [P, F16_PACK], F16)
        wreg = sb("wdec_region", [P, RANK * (D + 1)])
        xo = sb("x_then_o", [P, NC, KD, CH])
        xo_hi = sb("xo_hi", [P, NC, KD, CH], F32R)
        xo_lo = sb("xo_lo", [P, NC, KD, CH], F32R)
        w_hl = sb("w_hl", [P, E + 1, 2, EW], F32R)
        cw_hl = sb("cw_hl", [P, BATCH, 2, KD * D], F32R)
        gate_hl = sb("gate_hl", [P, KD, E, 2], F32R)
        u_sb = sb("u_sb", [P, BATCH, KD, RANK])
        u_last = sb("u_last", [RANK, BATCH])
        ut_sb = sb("ut_sb", [RANK, BATCH * D])
        bias = sb("bias", [P, KD, BATCH])
        orow = sb("orow", [P, 2, 2, D])
        relu = sb("relu", [P, 2 * H])
        hid = sb("hid", [P, 2 * H])
        xs_hl = sb("xs_hl", [P, 2, 2, KD, P], F32R)
        ht_hl = sb("ht_hl", [P, 2, 2, KD, P], F32R)
        sh_hl = sb("sh_hl", [P, 2, KD, CH], F32R)
        lg = sb("logits", [P, G, GJ, E])
        biased = sb("biased", [P, 2, GJ, E])
        best = sb("best", [P, 2, GJ])
        score = sb("score", [P, GJ, E])
        top_score = sb("top_score", [P, GJ])
        sel = sb("sel", [P, G, 2, GJ, E])
        mask16 = sb("mask16", [P, G, GJ, E], F16)
        msum16 = sb("msum16", [P, G, E], F16)
        ntile_i = sb("ntile_i", [P, E], I32)
        scan = sb("scan", [P, 4, 4 + E])
        slot_e = sb("slot_e", [P, GJ, E])
        picked = sb("picked", [P, 2, GJ, E])
        slot = sb("slot", [P, 2, GJ])
        tile_i = sb("tile_i", [P, 2, GJ], I32)
        tile_f = sb("tile_f", [P, 2, GJ])
        lane_f = sb("lane_f", [P, 2, GJ])
        oh_tile = sb("oh_tile", [P, 2 * GJ, GT], F16)
        oh_token = sb("oh_token", [P, 2 * GJ, GT], F16)
        oh_lane = sb("oh_lane", [P, 2 * GJ, P], F16)
        owner_cmp = sb("owner_cmp", [1, GT, E])
        owner_f = sb("owner_f", [1, GT])
        owner = sb("owner", [1, NT], I32)
        token_of = sb("token_of", [P, NT], I32)
        slot_i = sb("slot_i", [P, G, 2, GJ], I32)
        gate_s = sb("gate_s", [P, G, GJ * E])
        wsum = sb("wsum", [P, GJ])
        wgt = sb("wgt", [P, G, 2, GJ])

        stage = wreg[:, 0:STAGE * EW].rearrange("p (s w) -> p s w", s=STAGE)
        acc = wreg[:, 0:N // P * D].rearrange("p (j d) -> p j d", d=D)
        at = N // P * D
        xs = wreg[:, at:at + RING * 2 * D].rearrange("p (r t d) -> p r t d", r=RING, t=2)
        at += RING * 2 * D
        y_sb = wreg[:, at:at + RING * 2 * D].rearrange("p (r t d) -> p r t d", r=RING, t=2)
        fin_xo = xo[:, :, :, :].rearrange("p c k n -> p (c k n)")
        fin_at = N // P * D
        fin_fit = (RANK * (D + 1) - fin_at) // (2 * D)

        def fin(g, j, c):
            if g == 0:
                return fin_xo[:, (2 * j + c) * D:(2 * j + c + 1) * D]
            if j < fin_fit:
                return wreg[:, fin_at + (2 * j + c) * D:fin_at + (2 * j + c + 1) * D]
            return orow[:, j - fin_fit, c, :]

        def col(name, rows=P):
            return pack[0:rows, COL[name][0]:COL[name][1]]

        tri = pack16[:, F16_TRI:F16_TRI + P]
        ones = pack16[:, F16_ONES:F16_ONES + P]
        iota_lane = pack16[:, F16_IOTA:F16_IOTA + P]
        iota_tile = pack16[:, F16_TILE:F16_TILE + GT]
        ident = col("ident")

        bank = [ctx.enter_context(nc.psum_tensor(f"bank{i}", [P, 512], F32)) for i in range(8)]
        route_ps = bank[0:2]
        pair_ps = bank[2:4]
        cond_ps = bank[4:8]
        x_ps, z_ps, ht_ps, y_ps = bank[4:8]
        out_ps = bank[6:8]

        small_loaded = sem("small_loaded")
        wdec_loaded = [sem(f"wdec_loaded{i}") for i in range(WCH)]
        x_loaded = [sem(f"x_loaded{c}") for c in range(NC)]
        stage_loaded = [sem(f"stage_loaded{i}") for i in range(STAGE)]
        xrows_loaded = sem("xrows_loaded")
        rows_written = [[sem(f"rows_written{g}{r}") for r in range(2)] for g in range(G)]
        gathered = [sem(f"gathered{r}") for r in range(RING)]
        y_written = [sem(f"y_written{r}") for r in range(RING)]
        edge_written = sem("edge_written")
        fin_loaded = [sem(f"fin_loaded{j}") for j in range(GJ)]
        out_written = sem("out_written")
        decoded = sem("decoded")
        ut_done = sem("ut_done")
        param_done = sem("param_done")
        cond_done = sem("cond_done")
        logits_done = sem("logits_done")
        rows_done = sem("rows_done")
        counts_done = sem("counts_done")
        token_done = sem("token_done")
        sh1_done = sem("sh1_done")
        sh2_done = sem("sh2_done")
        xt_done = sem("xt_done")
        z_done = sem("z_done")
        htr_done = sem("htr_done")
        yps_done = sem("yps_done")
        x_hi = sem("x_hi")
        gate_hi = sem("gate_hi")
        ut_copied = sem("ut_copied")
        cw_hi = sem("cw_hi")
        w_hi = sem("w_hi")
        o_hi = sem("o_hi")
        rows_copied = sem("rows_copied")
        relu_done = sem("relu_done")
        sh_hi = sem("sh_hi")
        xs_hi = sem("xs_hi")
        ht_hi = sem("ht_hi")
        y_copied = sem("y_copied")
        sigmoid_done = sem("sigmoid_done")
        x_lo = sem("x_lo")
        gate_lo = sem("gate_lo")
        u_ready = sem("u_ready")
        cw_lo = sem("cw_lo")
        bias_ready = sem("bias_ready")
        o_ready = sem("o_ready")
        o_lo = sem("o_lo")
        route_step = sem("route_step")
        lg_ready = sem("lg_ready")
        mask_ready = sem("mask_ready")
        onehot_ready = sem("onehot_ready")
        token_ready = sem("token_ready")
        squared = sem("squared")
        sh_lo = sem("sh_lo")
        xs_lo = sem("xs_lo")
        ht_lo = sem("ht_lo")
        acc_ready = sem("acc_ready")
        half_ready = sem("half_ready")
        out_ready = sem("out_ready")
        x_lo_pool = sem("x_lo_pool")
        w_lo = sem("w_lo")

        DVE_X = 2
        GAP = 2
        LAST = NQ - 1
        HEAD = 2 + RING
        LOOPS = (NQ - HEAD - 1) // RING
        TAIL = range(HEAD + RING * LOOPS, NQ)
        BOUNDARY = (GT - 1) // 2
        assert GT % 2 == 1 and 0 < LOOPS and NT % 2 == 0 and GJ * 2 * 256 == NC * KD * CH

        def for_pairs(engine, body):
            for q in range(HEAD):
                body(q, q % RING, q // RING)
            with engine.Fori(0, LOOPS) as i:
                for q0 in range(HEAD, HEAD + RING):
                    body(RING * i + q0, q0 % RING, i + q0 // RING)
            for q in TAIL:
                body(q, q % RING, q // RING)

        def is_first(q):
            return isinstance(q, int) and q == 0

        def is_last(q):
            return isinstance(q, int) and q == LAST

        block = ctx.enter_context(nc.Block())

        @block.sync
        def _(sp):
            sp.dma_start(pack[:, :], small).then_inc(small_loaded, 16)
            sp.dma_start(pack16[:, :], small16).then_inc(small_loaded, 16)
            width = WK * (D + 1)
            for i in range(WCH):
                if i == WCH - 1:
                    sp.dma_start(xo[:, 0, :, :], xT[0]).then_inc(x_loaded[0], 16)
                sp.dma_start(wreg[:, i * width:(i + 1) * width],
                             wdec[:, i * width:(i + 1) * width]).then_inc(wdec_loaded[i], 16)
            for c in range(1, NC):
                sp.dma_start(xo[:, c, :, :], xT[c]).then_inc(x_loaded[c], 16)
            sp.wait_ge(decoded, 1)
            for n in range(E + 1):
                if n >= STAGE:
                    sp.wait_ge(w_hi, n - STAGE + 1)
                    sp.wait_ge(w_lo, n - STAGE + 1)
                e = (n + E) % (E + 1)
                sp.dma_start(stage[:, n % STAGE, :], experts[e]).then_inc(stage_loaded[n % STAGE], 16)
            sp.wait_ge(w_hi, E + 1)
            sp.wait_ge(w_lo, E + 1)
            sp.dma_start(acc, xrows_v).then_inc(xrows_loaded, 16)

            def write_y(g, q, r, n, written=None):
                sp.wait_ge(y_copied, n)
                sp.dma_start(y_v[g][bass.ds(q - g * BOUNDARY, 1)].rearrange("a p t d -> p (a t) d"),
                             y_sb[:, r, :, :]).then_inc(y_written[r] if written is None else written, 16)

            def write_all(g, first, end):
                loops = (end - first) // RING
                with sp.Fori(0, loops) as i:
                    for u in range(RING):
                        write_y(g, RING * i + (first + u), (first + u) % RING, RING * i + (first + u + 1))
                for q in range(first + RING * loops, end):
                    write_y(g, q, q % RING, q + 1)

            write_all(0, 0, BOUNDARY)
            write_y(1, BOUNDARY, BOUNDARY % RING, BOUNDARY + 1, edge_written)
            sp.wait_ge(edge_written, 16)
            write_y(0, BOUNDARY, BOUNDARY % RING, BOUNDARY + 1)
            write_all(1, BOUNDARY + 1, NQ)
            for g in range(G):
                for j in range(GJ):
                    sp.wait_ge(out_ready, g * GJ + j + 1)
                    t0 = (g * GJ + j) * P
                    sp.dma_start(out[t0:t0 + P, :], fin(g, j, 1)).then_inc(out_written, 16)
            sp.wait_ge(out_written, 16 * G * GJ)

        @block.gpsimd
        def _(pool):
            for c in range(DVE_X, NC):
                pool.wait_ge(x_hi, c + 1)
                nc.gpsimd.tensor_tensor(xo_lo[:, c, :, :], xo[:, c, :, :], xo_hi[:, c, :, :].bitcast(F32),
                                        ALU.subtract).then_inc(x_lo_pool, 1)
            for n in range(E + 1):
                e = (n + E) % (E + 1)
                pool.wait_ge(w_hi, n + 1)
                nc.gpsimd.tensor_tensor(w_hl[:, e, 1, :], stage[:, n % STAGE, :], w_hl[:, e, 0, :].bitcast(F32),
                                        ALU.subtract).then_inc(w_lo, 1)

            def writes(r, pairs):
                return 16 * len(range(r, pairs, RING))

            def gather_y(g, j):
                for c in range(2):
                    nc.gpsimd.indirect_dma_start(
                        out=fin(g, j, c), out_offset=None, in_=y_dram[g],
                        in_offset=bass.IndirectOffsetOnAxis(ap=slot_i[:, g, c, j:j + 1], axis=0),
                    ).then_inc(fin_loaded[j], 16)

            pending = [(0, j) for j in range(GJ)]
            for q in range(NQ):
                for t in range(2):
                    s = 2 * q + t
                    g = s // GT
                    if s % GT == 0:
                        pool.wait_ge(token_ready, g + 1)
                        for r in range(2):
                            pool.wait_ge(rows_written[g][r], 16 * (GJ // 4))
                    if t == 0 and q >= RING:
                        pool.wait_ge(xt_done, q - RING + 1)
                    nc.gpsimd.indirect_dma_start(
                        out=xs[:, q % RING, t, :], out_offset=None, in_=rows_dram[g],
                        in_offset=bass.IndirectOffsetOnAxis(ap=token_of[:, s:s + 1], axis=0),
                    ).then_inc(gathered[q % RING], 16)
                if q >= BOUNDARY + 6 and pending:
                    if pending[0] == (0, 0):
                        for r in range(RING):
                            pool.wait_ge(y_written[r], writes(r, BOUNDARY + 1))
                        pool.wait_ge(token_done, G)
                        pool.wait_ge(rows_done, G * GJ // 2)
                        pool.wait_ge(o_lo, NC)
                    for _ in range(2):
                        if pending:
                            gather_y(*pending.pop(0))
            while pending:
                gather_y(*pending.pop(0))
            for r in range(RING):
                pool.wait_ge(y_written[r], writes(r, NQ))
            for j in range(GJ):
                gather_y(1, j)

        @block.tensor
        def _(pe):
            mm = nc.tensor.matmul

            def split_product(dst, terms):
                last = None
                for n, ((s_hi, s_lo), (m_hi, m_lo)) in enumerate(terms):
                    mm(dst, s_hi, m_hi, start=(n == 0), stop=False)
                    mm(dst, s_hi, m_lo, start=False, stop=False)
                    last = mm(dst, s_lo, m_hi, start=False, stop=(n == len(terms) - 1))
                return last

            pe.wait_ge(small_loaded, 32)
            u_ps = route_ps[0][:, 0:KD * RANK * BATCH].rearrange("p (h k b) -> p h k b", h=KD, b=BATCH)
            for i in range(WCH):
                pe.wait_ge(wdec_loaded[i], 16)
                for k in range(i * WK, (i + 1) * WK):
                    for h in range(KD):
                        mm(u_ps[:, h, k, :], wreg[:, k * (D + 1) + h * P:k * (D + 1) + (h + 1) * P],
                           col("mu"), start=True, stop=True)
            w_last = wreg[:, :].rearrange("p (k i) -> p k i", i=D + 1)[:, :, D]
            mm(route_ps[1][0:RANK, 0:BATCH], w_last, col("mu"), start=True, stop=True).then_inc(decoded, 1)
            pe.wait_ge(u_ready, 2)
            for b in range(BATCH):
                for h in range(KD):
                    last = nc.tensor.transpose(route_ps[1][0:RANK, (b * KD + h) * P:(b * KD + h + 1) * P],
                                               u_sb[:, b, h, :], ident)
            last.then_inc(ut_done, 1)
            for m in range(KD):
                last = mm(cond_ps[0][:, m * BATCH:(m + 1) * BATCH],
                          col("V", RANK)[:, m * P:(m + 1) * P], u_last[:, :], start=True, stop=True)
            last.then_inc(param_done, 1)
            pe.wait_ge(ut_copied, 1)
            for b in range(BATCH):
                for h in range(KD):
                    last = mm(pair_ps[b][:, h * D:(h + 1) * D],
                              ut_sb[:, (b * KD + h) * P:(b * KD + h + 1) * P], col("V", RANK),
                              start=True, stop=True)
                last.then_inc(param_done, 1)

            def cond(c):
                b = c * CH // SEQ
                pe.wait_ge(x_hi, c + 1)
                if c < DVE_X:
                    pe.wait_ge(x_lo, c + 1)
                else:
                    pe.wait_ge(x_lo_pool, c + 1 - DVE_X)
                pe.wait_ge(cw_hi, b + 1)
                pe.wait_ge(cw_lo, b + 1)
                if c == 0:
                    pe.wait_ge(bias_ready, 1)
                for m in range(KD):
                    n = KD * c + m
                    if n >= 4:
                        pe.wait_ge(o_ready, n - 3)
                    terms = [((cw_hl[:, b, 0, k * D + m * P:k * D + (m + 1) * P],
                               cw_hl[:, b, 1, k * D + m * P:k * D + (m + 1) * P]),
                              (xo_hi[:, c, k, :], xo_lo[:, c, k, :])) for k in range(KD)]
                    split_product(cond_ps[n % 4][:, :], terms).then_inc(cond_done, 1)

            def logits(g):
                pe.wait_ge(gate_hi, 1)
                pe.wait_ge(gate_lo, 1)
                for j in range(GJ):
                    c, t = (g * GJ + j) // CT, (g * GJ + j) % CT
                    if t == 0:
                        pe.wait_ge(o_lo, c + 1)
                    n = 0
                    for k in range(KD):
                        for part in (xo_hi, xo_lo):
                            last = mm(route_ps[g][:, j * 2 * E:(j + 1) * 2 * E],
                                      part[:, c, k, t * P:(t + 1) * P],
                                      gate_hl[:, k, :, :].rearrange("p e s -> p (e s)"),
                                      start=(n == 0), stop=(n == 2 * KD - 1))
                            n += 1
                last.then_inc(logits_done, 1)

            def rows(g):
                for n in range(g * GJ // 2, (g + 1) * GJ // 2):
                    if n < 2:
                        pe.wait_ge(cw_lo, n + 1)
                    else:
                        pe.wait_ge(rows_copied, n - 1)
                    for t in range(2):
                        c, tt = (2 * n + t) // CT, (2 * n + t) % CT
                        for k in range(KD):
                            last = nc.tensor.transpose(pair_ps[n % 2][:, t * D + k * P:t * D + (k + 1) * P],
                                                       xo[:, c, k, tt * P:(tt + 1) * P], ident)
                    last.then_inc(rows_done, 1)

            def counts(g):
                pe.wait_ge(mask_ready, g + 1)
                cnt = route_ps[g][:, 0:GJ * E]
                flat = mask16[:, g, :, :].rearrange("p j e -> p (j e)")
                mm(cnt, tri, flat, start=True, stop=False)
                for j in range(GJ - 1):
                    later = GJ - 1 - j
                    mm(route_ps[g][:, (j + 1) * E:GJ * E].rearrange("p (j e) -> p j e", e=E), ones,
                       mask16[:, g, j:j + 1, :].to_broadcast([P, later, E]),
                       start=False, stop=(j == GJ - 2))
                mm(route_ps[g][:, GJ * E:(GJ + 1) * E], ones, msum16[:, g, :],
                   start=True, stop=True).then_inc(counts_done, 1)

            def tokens(g):
                for n in range(2 * GJ):
                    pe.wait_ge(onehot_ready, g * (2 * GJ + 1) + n + 2)
                    last = mm(route_ps[g][:, 0:GT], oh_lane[:, n, :], oh_token[:, n, :],
                              start=(n == 0), stop=(n == 2 * GJ - 1))
                last.then_inc(token_done, 1)

            def w_part(e, part, layer, k, m=None):
                lo = layer * KD * H + k * D
                return w_hl[:, e, part, lo:lo + D] if m is None else w_hl[:, e, part, lo + m * P:lo + (m + 1) * P]

            def shared_first(c):
                if c == 0:
                    pe.wait_ge(w_hi, 1)
                    pe.wait_ge(w_lo, 1)
                pe.wait_ge(o_lo, c + 1)
                for m in range(KD):
                    n = KD * c + m
                    if n < 2:
                        pe.wait_ge(rows_copied, G * GJ // 2)
                    else:
                        pe.wait_ge(squared, (n - 1) if n < KD * GAP + 2 else (n - 1) + NQ)
                    terms = [((w_part(E, 0, 0, k, m), w_part(E, 1, 0, k, m)),
                              (xo_hi[:, c, k, :], xo_lo[:, c, k, :])) for k in range(KD)]
                    split_product(pair_ps[n % 2][:, :], terms).then_inc(sh1_done, 1)

            def shared_second(c):
                pe.wait_ge(sh_hi, KD * (c + 1))
                pe.wait_ge(sh_lo, KD * (c + 1))
                for v in range(2):
                    n = 2 * c + v
                    if n < 2:
                        pe.wait_ge(o_ready, KD * NC)
                    elif n in (2 * GAP, 2 * GAP + 1):
                        pe.wait_ge(ht_lo, NQ)
                        pe.wait_ge(y_copied, NQ)
                    else:
                        pe.wait_ge(acc_ready, n - 1)
                    for t in range(2):
                        at_ = (2 * v + t) * P
                        terms = [((sh_hl[:, 0, k, at_:at_ + P], sh_hl[:, 1, k, at_:at_ + P]),
                                  (w_part(E, 0, 1, k), w_part(E, 1, 1, k))) for k in range(KD)]
                        last = split_product(out_ps[n % 2][:, t * D:(t + 1) * D], terms)
                    last.then_inc(sh2_done, 1)

            for c in range(GC + 1):
                cond(c)
            logits(0)
            rows(0)
            for c in range(GC + 1, NC):
                cond(c)
            logits(1)
            rows(1)
            counts(0)
            shared_first(0)
            tokens(0)
            shared_second(0)
            counts(1)
            shared_first(1)
            tokens(1)
            shared_second(1)

            def expert_of(s):
                return pe.value_load(owner[0:1, bass.ds(s, 1)], min_val=0, max_val=E - 1)

            def dyn_w(e, part, layer, k):
                lo = layer * KD * H + k * D
                return w_hl[:, bass.ds(e, 1), part, lo:lo + D]

            def transpose_x(r, n_gathered):
                pe.wait_ge(gathered[r], 32 * n_gathered)
                for t in range(2):
                    for k in range(KD):
                        last = nc.tensor.transpose(x_ps[:, (t * KD + k) * P:(t * KD + k + 1) * P],
                                                   xs[:, r, t, k * P:(k + 1) * P], ident)
                last.then_inc(xt_done, 1)

            def first_layer(experts_, q):
                pe.wait_ge(xs_lo, q + 1)
                pe.wait_ge(squared, KD * GAP + q)
                for t in range(2):
                    terms = [((xs_hl[:, 0, t, k, :], xs_hl[:, 1, t, k, :]),
                              (dyn_w(experts_[t], 0, 0, k), dyn_w(experts_[t], 1, 0, k))) for k in range(KD)]
                    last = split_product(z_ps[:, t * H:(t + 1) * H], terms)
                last.then_inc(z_done, 1)

            def second_layer(experts_, q):
                pe.wait_ge(ht_lo, q + 1)
                if not is_first(q):
                    pe.wait_ge(y_copied, q)
                for t in range(2):
                    terms = [((ht_hl[:, 0, t, k, :], ht_hl[:, 1, t, k, :]),
                              (dyn_w(experts_[t], 0, 1, k), dyn_w(experts_[t], 1, 1, k))) for k in range(KD)]
                    last = split_product(y_ps[:, t * D:(t + 1) * D], terms)
                last.then_inc(yps_done, 1)

            def transpose_h(q):
                pe.wait_ge(squared, KD * GAP + q + 1)
                for t in range(2):
                    for k in range(KD):
                        last = nc.tensor.transpose(ht_ps[:, (t * KD + k) * P:(t * KD + k + 1) * P],
                                                   hid[:, t * H + k * P:t * H + (k + 1) * P], ident)
                last.then_inc(htr_done, 1)

            pe.wait_ge(w_lo, E + 1)
            pe.wait_ge(o_ready, KD * NC)
            pe.wait_ge(acc_ready, 2 * GAP)
            transpose_x(0, 1)

            def tile_pair(q, slot, turn):
                first_layer([expert_of(2 * q + t) for t in range(2)], q)
                if not is_last(q):
                    transpose_x((slot + 1) % RING, turn + (slot + 1) // RING + 1)
                if not is_first(q):
                    second_layer([expert_of(2 * (q - 1) + t) for t in range(2)], q - 1)
                transpose_h(q)

            for_pairs(pe, tile_pair)
            second_layer([expert_of(2 * LAST + t) for t in range(2)], LAST)
            for c in range(GAP, NC):
                shared_first(c)
                shared_second(c)

        @block.scalar
        def _(act):
            copy = nc.scalar.activation

            def split_x(c):
                act.wait_ge(x_loaded[c], 16)
                copy(xo_hi[:, c, :, :], xo[:, c, :, :], ACT.Copy).then_inc(x_hi, 1)

            def split_w(n):
                e = (n + E) % (E + 1)
                act.wait_ge(stage_loaded[n % STAGE], 16 * (n // STAGE + 1))
                copy(w_hl[:, e, 0, :], stage[:, n % STAGE, :], ACT.Copy).then_inc(w_hi, 1)

            def split_o(c):
                act.wait_ge(o_ready, KD * (c + 1))
                copy(xo_hi[:, c, :, :], xo[:, c, :, :], ACT.Copy).then_inc(o_hi, 1)

            def copy_rows(n):
                g = 2 * n // GJ
                act.wait_ge(rows_done, n + 1)
                if n >= 2:
                    act.wait_ge(rows_written[2 * (n - 2) // GJ][n % 2], 16 * ((n - 2) % (GJ // 2) // 2 + 1))
                copy(orow[:, n % 2, :, :], pair_ps[n % 2][:, :].rearrange("p (t d) -> p t d", d=D),
                     ACT.Copy).then_inc(rows_copied, 1)
                act.wait_ge(rows_copied, n + 1)
                act.dma_start(rows_v[g][n % (GJ // 2)], orow[:, n % 2, :, :]).then_inc(rows_written[g][n % 2], 16)

            def relu_unit(ps, produced, n_produced, n_squared):
                act.wait_ge(produced, n_produced)
                if n_squared is not None:
                    act.wait_ge(squared, n_squared)
                copy(relu[:, :], ps[:, :], ACT.Relu).then_inc(relu_done, 1)

            def split_shared(c, m, n):
                act.wait_ge(squared, n + 1)
                if c >= 1:
                    act.wait_ge(sh2_done, 2 * c)
                copy(sh_hl[:, 0, m, :], hid[:, :], ACT.Copy).then_inc(sh_hi, 1)

            act.wait_ge(small_loaded, 32)
            copy(gate_hl[:, :, :, 0], col("gate").rearrange("p (k e) -> p k e", e=E), ACT.Copy).then_inc(gate_hi, 1)
            split_x(0)
            act.wait_ge(ut_done, 1)
            copy(ut_sb[:, :], route_ps[1][0:RANK, 0:BATCH * D], ACT.Copy).then_inc(ut_copied, 1)
            for b in range(BATCH):
                act.wait_ge(param_done, b + 2)
                copy(cw_hl[:, b, 0, :], pair_ps[b][:, :], ACT.Copy).then_inc(cw_hi, 1)
            for c in range(1, NC):
                split_x(c)
            w_n = 0
            for c in range(GC):
                split_o(c)
                for _ in range(1):
                    split_w(w_n)
                    w_n += 1
            split_o(GC)
            for n in range(GJ // 2):
                copy_rows(n)
            for c in range(GC + 1, NC):
                split_w(w_n)
                w_n += 1
                split_o(c)
            for n in range(GJ // 2, GJ):
                copy_rows(n)
            act.wait_ge(lg_ready, 1)
            copy(gate_s[:, 0, :], lg[:, 0, :, :].rearrange("p j e -> p (j e)"), ACT.Sigmoid).then_inc(sigmoid_done, 1)
            for c in range(GAP):
                for m in range(KD):
                    n = KD * c + m
                    relu_unit(pair_ps[n % 2], sh1_done, n + 1, n if n else None)
                    split_shared(c, m, n)
                    if w_n <= E:
                        split_w(w_n)
                        w_n += 1
            while w_n <= E:
                split_w(w_n)
                w_n += 1
            act.wait_ge(lg_ready, 2)
            copy(gate_s[:, 1, :], lg[:, 1, :, :].rearrange("p j e -> p (j e)"), ACT.Sigmoid).then_inc(sigmoid_done, 1)

            def split_xs(q):
                act.wait_ge(xt_done, q + 1)
                if not is_first(q):
                    act.wait_ge(z_done, q)
                copy(xs_hl[:, 0, :, :, :].rearrange("p t k n -> p (t k n)"), x_ps[:, :], ACT.Copy).then_inc(xs_hi, 1)

            def split_ht(q):
                act.wait_ge(htr_done, q + 1)
                if not is_first(q):
                    act.wait_ge(yps_done, q)
                copy(ht_hl[:, 0, :, :, :].rearrange("p t k n -> p (t k n)"), ht_ps[:, :], ACT.Copy).then_inc(ht_hi, 1)

            def copy_y(q, slot, turn):
                act.wait_ge(yps_done, q + 1)
                if not isinstance(turn, int) or turn > 0:
                    act.wait_ge(y_written[slot], 16 * turn)
                copy(y_sb[:, slot, :, :].rearrange("p t d -> p (t d)"), y_ps[:, :], ACT.Copy).then_inc(y_copied, 1)

            UNITS = KD * GAP

            def tile_pair(q, slot, turn):
                relu_unit(z_ps, z_done, q + 1, q + UNITS)
                if not is_last(q):
                    split_xs(q + 1)
                if not is_first(q):
                    copy_y(q - 1, (slot - 1) % RING, turn if slot else turn - 1)
                split_ht(q)

            split_xs(0)
            for_pairs(act, tile_pair)
            copy_y(LAST, LAST % RING, LAST // RING)
            for c in range(GAP, NC):
                for m in range(KD):
                    n = KD * c + m
                    relu_unit(pair_ps[n % 2], sh1_done, n + 1, n + NQ)
                    split_shared(c, m, n + NQ)

        @block.vector
        def _(dve):
            tt, ts, stt, red = (nc.vector.tensor_tensor, nc.vector.tensor_scalar,
                                nc.vector.scalar_tensor_tensor, nc.vector.tensor_reduce)
            steps = [0]

            def step(ins):
                ins.then_inc(route_step, 1)
                steps[0] += 1
                dve.wait_ge(route_step, steps[0])

            def split_x(c):
                dve.wait_ge(x_hi, c + 1)
                tt(xo_lo[:, c, :, :], xo[:, c, :, :], xo_hi[:, c, :, :].bitcast(F32), ALU.subtract).then_inc(x_lo, 1)

            def add_bias(c):
                b = c * CH // SEQ
                for m in range(KD):
                    dve.wait_ge(cond_done, KD * c + KD)
                    ts(xo[:, c, m, :], cond_ps[(KD * c + m) % 4][:, :], bias[:, m, b:b + 1], None,
                       ALU.add).then_inc(o_ready, 1)

            def split_o(c):
                dve.wait_ge(o_hi, c + 1)
                tt(xo_lo[:, c, :, :], xo[:, c, :, :], xo_hi[:, c, :, :].bitcast(F32), ALU.subtract).then_inc(o_lo, 1)

            def choose(g):
                dve.wait_ge(logits_done, g + 1)
                red(lg[:, g, :, :], route_ps[g][:, 0:GJ * 2 * E].rearrange("p (j e s) -> p j e s", e=E, s=2),
                    X_AXIS, ALU.add).then_inc(lg_ready, 1)
                dve.wait_ge(lg_ready, g + 1)
                step(tt(biased[:, 0, :, :], lg[:, g, :, :],
                        col("lb").unsqueeze(1).to_broadcast([P, GJ, E]), ALU.add))
                for c in range(2):
                    step(red(best[:, c, :], biased[:, c, :, :], X_AXIS, ALU.max))
                    step(tt(score[:, :, :], biased[:, c, :, :],
                            best[:, c, :].unsqueeze(2).to_broadcast([P, GJ, E]), ALU.is_equal))
                    step(tt(score[:, :, :], score[:, :, :],
                            col("rank_score").unsqueeze(1).to_broadcast([P, GJ, E]), ALU.mult))
                    step(red(top_score[:, :], score[:, :, :], X_AXIS, ALU.max))
                    step(tt(sel[:, g, c, :, :], score[:, :, :],
                            top_score[:, :].unsqueeze(2).to_broadcast([P, GJ, E]), ALU.is_equal))
                    if c == 0:
                        step(stt(biased[:, 1, :, :], sel[:, g, 0, :, :], -BIG, biased[:, 0, :, :],
                                 ALU.mult, ALU.add))
                step(tt(mask16[:, g, :, :], sel[:, g, 0, :, :], sel[:, g, 1, :, :], ALU.add))
                with nc.allow_low_precision(reason="sums of at most 8 ones are exact in float16"):
                    red(msum16[:, g, :], mask16[:, g, :, :].rearrange("p j e -> p e j"), X_AXIS,
                        ALU.add).then_inc(mask_ready, 1)

            def place(g):
                dve.wait_ge(counts_done, g + 1)
                step(ts(ntile_i[:, :], route_ps[g][:, GJ * E:(GJ + 1) * E], 1.0 / P,
                        (P - 1) / P - (P - 1) / (2 * P), ALU.mult, ALU.add))
                step(nc.vector.tensor_copy(scan[:, 0, 4:], ntile_i[:, :]))
                for n, d in enumerate((1, 2, 4)):
                    step(tt(scan[:, n + 1, 4:], scan[:, n, 4:], scan[:, n, 4 - d:4 + E - d], ALU.add))
                ends = scan[:, 3, 4:]
                step(tt(scan[:, 1, 4:], ends, scan[:, 0, 4:], ALU.subtract))
                step(stt(slot_e[:, :, :], scan[:, 1, 4:].unsqueeze(1).to_broadcast([P, GJ, E]), float(P),
                         route_ps[g][:, 0:GJ * E].rearrange("p (j e) -> p j e", e=E), ALU.mult, ALU.add))
                step(tt(picked[:, :, :, :].rearrange("p c j e -> p c (j e)"),
                        sel[:, g, :, :, :].rearrange("p c j e -> p c (j e)"),
                        slot_e[:, :, :].rearrange("p j e -> p (j e)").unsqueeze(1).to_broadcast([P, 2, GJ * E]),
                        ALU.mult))
                step(red(slot[:, :, :], picked[:, :, :, :], X_AXIS, ALU.add))
                step(ts(tile_i[:, :, :], slot[:, :, :], 1.0 / P, -(P - 1) / (2 * P), ALU.mult, ALU.add))
                step(nc.vector.tensor_copy(tile_f[:, :, :], tile_i[:, :, :]))
                step(stt(lane_f[:, :, :], tile_f[:, :, :], -float(P), slot[:, :, :], ALU.mult, ALU.add))
                if g:
                    dve.wait_ge(token_done, g)
                step(tt(oh_tile[:, :, :], iota_tile.unsqueeze(1).to_broadcast([P, 2 * GJ, GT]),
                        tile_f[:, :, :].rearrange("p c j -> p (c j)").unsqueeze(2).to_broadcast([P, 2 * GJ, GT]),
                        ALU.is_equal))
                token = col("token")
                tt(oh_token[:, :, :].rearrange("p (c j) n -> p c j n", c=2),
                   oh_tile[:, :, :].rearrange("p (c j) n -> p c j n", c=2),
                   token.unsqueeze(1).unsqueeze(3).to_broadcast([P, 2, GJ, GT]), ALU.mult).then_inc(onehot_ready, 1)
                for n in range(2 * GJ):
                    ts(oh_lane[:, n, :], iota_lane, lane_f[:, n // GJ, n % GJ:n % GJ + 1], None,
                       ALU.is_equal).then_inc(onehot_ready, 1)
                step(tt(owner_cmp[:, :, :],
                        pack[0:1, COL["tile_no"][0]:COL["tile_no"][1]].unsqueeze(2).to_broadcast([1, GT, E]),
                        scan[0:1, 3, 4:].unsqueeze(1).to_broadcast([1, GT, E]), ALU.is_ge))
                step(red(owner_f[:, :], owner_cmp[:, :, :], X_AXIS, ALU.add))
                step(ts(owner[:, g * GT:(g + 1) * GT], owner_f[:, :], float(E - 1), None, ALU.min))
                step(ts(slot_i[:, g, :, :], slot[:, :, :], float(g * P), None, ALU.add))
                dve.wait_ge(token_done, g + 1)
                nc.vector.tensor_copy(token_of[:, g * GT:(g + 1) * GT], route_ps[g][:, 0:GT]).then_inc(token_ready, 1)

            def weights(g):
                dve.wait_ge(sigmoid_done, g + 1)
                step(tt(picked[:, :, :, :].rearrange("p c j e -> p c (j e)"),
                        sel[:, g, :, :, :].rearrange("p c j e -> p c (j e)"),
                        gate_s[:, g, :].unsqueeze(1).to_broadcast([P, 2, GJ * E]), ALU.mult))
                step(red(wgt[:, g, :, :], picked[:, :, :, :], X_AXIS, ALU.add))
                step(tt(wsum[:, :], wgt[:, g, 0, :], wgt[:, g, 1, :], ALU.add))
                step(ts(wsum[:, :], wsum[:, :], 1e-6, None, ALU.add))
                step(nc.vector.reciprocal(wsum[:, :], wsum[:, :]))
                step(tt(wgt[:, g, :, :], wgt[:, g, :, :], wsum[:, :].unsqueeze(1).to_broadcast([P, 2, GJ]), ALU.mult))

            def square(ps, n, n_free, free):
                dve.wait_ge(relu_done, n + 1)
                if free is not None:
                    dve.wait_ge(free, n_free)
                stt(hid[:, :], ps[:, :], 0.0, relu[:, :], ALU.max, ALU.mult).then_inc(squared, 1)

            def shared_unit(c, m, n, n_free, free):
                square(pair_ps[(KD * c + m) % 2], n, n_free, free)
                dve.wait_ge(sh_hi, KD * c + m + 1)
                tt(sh_hl[:, 1, m, :], hid[:, :], sh_hl[:, 0, m, :].bitcast(F32), ALU.subtract).then_inc(sh_lo, 1)

            def add_shared(n):
                dve.wait_ge(xrows_loaded, 16)
                dve.wait_ge(sh2_done, n + 1)
                tt(acc[:, 2 * n:2 * n + 2, :], out_ps[n % 2][:, :].rearrange("p (t d) -> p t d", d=D),
                   acc[:, 2 * n:2 * n + 2, :], ALU.add).then_inc(acc_ready, 1)

            dve.wait_ge(small_loaded, 32)
            dve.wait_ge(gate_hi, 1)
            tt(gate_hl[:, :, :, 1], col("gate").rearrange("p (k e) -> p k e", e=E),
               gate_hl[:, :, :, 0].bitcast(F32), ALU.subtract).then_inc(gate_lo, 1)
            step(nc.vector.memset(scan[:, :, :], 0.0))
            split_x(0)
            dve.wait_ge(decoded, 1)
            tt(u_sb[:, :, :, :].rearrange("p b h k -> p b (h k)"),
               route_ps[0][:, 0:KD * RANK * BATCH].rearrange("p (hk b) -> p b hk", b=BATCH),
               col("b_main").unsqueeze(1).to_broadcast([P, BATCH, KD * RANK]), ALU.add).then_inc(u_ready, 1)
            ts(u_last[:, :], route_ps[1][0:RANK, 0:BATCH], col("b_last", RANK), None, ALU.add).then_inc(u_ready, 1)
            dve.wait_ge(param_done, 1)
            nc.vector.tensor_copy(bias[:, :, :], cond_ps[0][:, 0:KD * BATCH].rearrange("p (m b) -> p m b", b=BATCH))\
                .then_inc(bias_ready, 1)
            for b in range(BATCH):
                dve.wait_ge(cw_hi, b + 1)
                tt(cw_hl[:, b, 1, :], pair_ps[b][:, :], cw_hl[:, b, 0, :].bitcast(F32), ALU.subtract)\
                    .then_inc(cw_lo, 1)
            for c in range(1, DVE_X):
                split_x(c)
            dve.wait_ge(bias_ready, 1)
            for c in range(GC + 1):
                add_bias(c)
                split_o(c)
            choose(0)
            for c in range(GC + 1, NC):
                add_bias(c)
                split_o(c)
            place(0)
            weights(0)
            choose(1)
            UNITS = KD * GAP
            for c in range(GAP):
                for m in range(KD):
                    n = KD * c + m
                    shared_unit(c, m, n, n, sh_lo if n else None)
            place(1)
            weights(1)
            for n in range(2 * GAP):
                add_shared(n)

            def split_xs(q):
                dve.wait_ge(xs_hi, q)
                tt(xs_hl[:, 1, :, :, :].rearrange("p t k n -> p (t k n)"), x_ps[:, :],
                   xs_hl[:, 0, :, :, :].rearrange("p t k n -> p (t k n)").bitcast(F32), ALU.subtract)\
                    .then_inc(xs_lo, 1)

            def split_ht(q):
                dve.wait_ge(ht_hi, q)
                tt(ht_hl[:, 1, :, :, :].rearrange("p t k n -> p (t k n)"), ht_ps[:, :],
                   ht_hl[:, 0, :, :, :].rearrange("p t k n -> p (t k n)").bitcast(F32), ALU.subtract)\
                    .then_inc(ht_lo, 1)

            def tile_pair(q, slot, turn):
                if is_first(q):
                    square(z_ps, UNITS, UNITS, sh_lo)
                else:
                    square(z_ps, q + UNITS, q, htr_done)
                if not is_last(q):
                    split_xs(q + 2)
                split_ht(q + 1)

            split_xs(1)
            for_pairs(dve, tile_pair)

            def combine(g, j):
                dve.wait_ge(fin_loaded[j], 32 * (g + 1))
                stt(fin(g, j, 0), fin(g, j, 0), wgt[:, g, 0, j:j + 1], acc[:, g * GJ + j, :],
                    ALU.mult, ALU.add).then_inc(half_ready, 1)
                dve.wait_ge(half_ready, g * GJ + j + 1)
                stt(fin(g, j, 1), fin(g, j, 1), wgt[:, g, 1, j:j + 1], fin(g, j, 0),
                    ALU.mult, ALU.add).then_inc(out_ready, 1)

            done = 0
            for c in range(GAP, NC):
                for m in range(KD):
                    n = KD * c + m
                    shared_unit(c, m, n + NQ, NQ if n == UNITS else n, htr_done if n == UNITS else sh_lo)
                    for _ in range(GJ // (KD * (NC - GAP))):
                        combine(0, done)
                        done += 1
                add_shared(2 * c)
                add_shared(2 * c + 1)
            for j in range(GJ):
                if j % 2 == 0:
                    dve.wait_ge(acc_ready, GJ // 2 + j // 2 + 1)
                combine(1, j)


def kernel(x, cond_512, L0_cond_W_dec, L0_cond_b_dec, L0_cond_V, L0_ffn_gate_w, L0_ffn_lb_bias,
           L0_ffn_w1, L0_ffn_w2, L0_ffn_cfc, L0_ffn_cproj):
    import numpy as np
    import concourse.bacc as bacc
    from concourse.bass_utils import run_bass_kernel_spmd

    def arr(a):
        return np.asarray(a)

    rows = arr(x).reshape(N, D)
    x_t = np.ascontiguousarray(rows.T.reshape(KD, P, NC, CH).transpose(2, 1, 0, 3))
    wdec = np.ascontiguousarray(arr(L0_cond_W_dec).reshape(MU, D + 1, RANK).transpose(0, 2, 1)).reshape(MU, -1)
    b_dec = arr(L0_cond_b_dec).reshape(D + 1, RANK)

    small = np.zeros((P, PACK), np.float32)

    def put(name, a):
        small[0:a.shape[0], COL[name][0]:COL[name][1]] = a

    put("mu", arr(cond_512).T)
    put("b_main", b_dec[:D].reshape(KD, P, RANK).transpose(1, 0, 2).reshape(P, -1))
    put("b_last", b_dec[D:].T)
    put("gate", arr(L0_ffn_gate_w).T.reshape(KD, P, E).transpose(1, 0, 2).reshape(P, -1))
    put("lb", np.tile(arr(L0_ffn_lb_bias), (P, 1)))
    put("V", arr(L0_cond_V))
    put("rank_score", np.tile(np.arange(E, 0, -1, dtype=np.float32), (P, 1)))
    put("token", (np.arange(GJ)[None, :] * P + np.arange(P)[:, None]).astype(np.float32))
    put("tile_no", np.tile(np.arange(GT, dtype=np.float32), (P, 1)))
    put("ident", np.eye(P, dtype=np.float32))
    small16 = np.zeros((P, F16_PACK), np.float16)
    small16[:, F16_TRI:F16_TRI + P] = np.triu(np.ones((P, P), np.float16), 1)
    small16[:, F16_ONES:F16_ONES + P] = 1
    small16[:, F16_IOTA:F16_IOTA + P] = np.arange(P)
    small16[:, F16_TILE:F16_TILE + GT] = np.arange(GT)

    def halves(w):
        return w.T.reshape(KD, P, -1).transpose(1, 0, 2).reshape(P, -1)

    first = [arr(L0_ffn_w1)[e] for e in range(E)] + [arr(L0_ffn_cfc)]
    second = [arr(L0_ffn_w2)[e] for e in range(E)] + [arr(L0_ffn_cproj)]
    experts = np.stack([np.concatenate([halves(a), halves(b)], axis=1) for a, b in zip(first, second)])

    arrays = {"small_dram": small, "small16_dram": small16, "wdec_dram": wdec, "xT_dram": x_t,
              "xrows_dram": np.ascontiguousarray(rows), "experts_dram": np.ascontiguousarray(experts)}
    nc = bacc.Bacc("TRN2", target_bir_lowering=False, num_devices=1)
    args = [nc.dram_tensor(k, a.shape, mybir.dt.from_np(a.dtype), kind="ExternalInput").ap()
            for k, a in arrays.items()]
    out = nc.dram_tensor("out_dram", (N, D), F32, kind="ExternalOutput").ap()
    build_moe(nc, *args, out)
    r = run_bass_kernel_spmd(nc, [arrays], core_ids=[0])
    return r.results[0]["out_dram"].reshape(BATCH, SEQ, D)
```

```python
from contextlib import ExitStack

import concourse.bass as bass
from concourse import mybir

F32 = mybir.dt.float32
F32R = mybir.dt.float32r
F16 = mybir.dt.float16
I32 = mybir.dt.int32
ALU = mybir.AluOpType
ACT = mybir.ActivationFunctionType
X_AXIS = mybir.AxisListType.X

P = 128
BATCH, SEQ, D = 2, 1024, 256
N = BATCH * SEQ
E, H = 8, 256
MU, RANK = 128, 30
KD = D // P
CH = 512
NC = N // CH
CT = CH // P
G = 2
GN = N // G
GJ = GN // P
GC = NC // G
GT = (2 * GN + E * (P - 1)) // P
NT = G * GT
NQ = NT // 2
RING = 3
LANE = 32
WK = P // LANE
WG = -(-RANK // WK)
EW = KD * H + KD * D
BIG = 3.0e38

_WIDTHS = [("gate", KD * E), ("lb", E), ("rank_score", E), ("token", GJ), ("tile_no", GT),
           ("b_dec", D + 1), ("ident", P), ("V", D)]
COL, _at = {}, 0
for _name, _width in _WIDTHS:
    COL[_name] = (_at, _at + _width)
    _at += _width
PACK = _at
F16_TRI, F16_ONES, F16_IOTA, F16_TILE, F16_PACK = 0, P, 2 * P, 3 * P, 3 * P + GT + GT % 2


def build_moe(nc, mu, small, small16, wdec, xT, xrows, experts, out):
    rows_dram = [nc.dram_tensor(f"cond_rows{g}", (GN, D), F32, kind="Internal").ap() for g in range(G)]
    y_dram = [nc.dram_tensor(f"expert_rows{g}", ((GT + 1) * P, D), F32, kind="Internal").ap() for g in range(G)]
    rows_v = [a.rearrange("(n t p) d -> n p t d", t=2, p=P) for a in rows_dram]
    y_v = [a.rearrange("(n t p) d -> n p t d", t=2, p=P) for a in y_dram]
    xrows_v = xrows.rearrange("(j p) d -> p j d", p=P)

    with ExitStack() as ctx:
        def sb(name, shape, dt=F32):
            return ctx.enter_context(nc.sbuf_tensor(name, shape, dt))

        def sem(name):
            return ctx.enter_context(nc.semaphore(name))

        mu_sb = sb("mu_sb", [P, LANE])
        pack = sb("pack", [P, PACK])
        pack16 = sb("pack16", [P, F16_PACK], F16)
        wreg = sb("wdec_region", [P, RANK * (D + 1)])
        xo = sb("x_then_o", [P, NC, KD, CH])
        xo_hi = sb("xo_hi", [P, NC, KD, CH], F32R)
        xo_lo = sb("xo_lo", [P, NC, KD, CH], F32R)
        w_hl = sb("w_hl", [P, E + 1, 2, EW], F32R)
        cw_hl = sb("cw_hl", [P, BATCH, 2, KD * D], F32R)
        gate_hl = sb("gate_hl", [P, KD, E, 2], F32R)
        ut_sb = sb("ut_sb", [RANK, BATCH, D + 1])
        bias = sb("bias", [P, KD, BATCH])
        scratch = sb("scratch", [P, WG * (D + 1)])
        u_rows = scratch[:, :].rearrange("p (g i) -> p g i", i=D + 1)
        relu = scratch[:, 0:2 * H]
        hid = scratch[:, 2 * H:4 * H]
        orow = scratch[:, 4 * H:4 * H + 4 * D].rearrange("p (s t d) -> p s t d", s=2, t=2)
        xs_hl = sb("xs_hl", [P, 2, 2, KD, P], F32R)
        ht_hl = sb("ht_hl", [P, 2, 2, KD, P], F32R)
        sh_hl = sb("sh_hl", [P, 2, KD, CH], F32R)
        lg = sb("logits", [P, G, GJ, E])
        biased = sb("biased", [P, 2, GJ, E])
        best = sb("best", [P, 2, GJ])
        score = sb("score", [P, GJ, E])
        top_score = sb("top_score", [P, GJ])
        sel = sb("sel", [P, G, 2, GJ, E])
        mask16 = sb("mask16", [P, G, GJ, E], F16)
        msum16 = sb("msum16", [P, G, E], F16)
        ntile_i = sb("ntile_i", [P, E], I32)
        scan = sb("scan", [P, 4, 4 + E])
        slot_e = sb("slot_e", [P, GJ, E])
        picked = sb("picked", [P, 2, GJ, E])
        slot = sb("slot", [P, 2, GJ])
        tile_i = sb("tile_i", [P, 2, GJ], I32)
        tile_f = sb("tile_f", [P, 2, GJ])
        lane_f = sb("lane_f", [P, 2, GJ])
        oh_tile = sb("oh_tile", [P, 2 * GJ, GT], F16)
        oh_token = sb("oh_token", [P, 2 * GJ, GT], F16)
        oh_lane = sb("oh_lane", [P, 2 * GJ, P], F16)
        owner_cmp = sb("owner_cmp", [1, GT, E])
        owner_f = sb("owner_f", [1, GT])
        owner = sb("owner", [1, NT], I32)
        token_of = sb("token_of", [P, NT], I32)
        slot_i = sb("slot_i", [P, G, 2, GJ], I32)
        gate_s = sb("gate_s", [P, G, GJ * E])
        wsum = sb("wsum", [P, GJ])
        wgt = sb("wgt", [P, G, 2, GJ])

        acc = wreg[:, 0:N // P * D].rearrange("p (j d) -> p j d", d=D)
        at = N // P * D
        xs = wreg[:, at:at + RING * 2 * D].rearrange("p (r t d) -> p r t d", r=RING, t=2)
        at += RING * 2 * D
        y_sb = wreg[:, at:at + RING * 2 * D].rearrange("p (r t d) -> p r t d", r=RING, t=2)
        STAGE = (at + RING * 2 * D - N // P * D) // EW
        stage = [wreg[:, N // P * D + (STAGE - 1 - n) * EW:N // P * D + (STAGE - n) * EW] for n in range(STAGE)]
        fin_xo = xo[:, :, :, :].rearrange("p c k n -> p (c k n)")
        fin_at = N // P * D
        fin_fit = (RANK * (D + 1) - fin_at) // (2 * D)

        def fin(g, j, c):
            if g == 0:
                return fin_xo[:, (2 * j + c) * D:(2 * j + c + 1) * D]
            if j < fin_fit:
                return wreg[:, fin_at + (2 * j + c) * D:fin_at + (2 * j + c + 1) * D]
            return orow[:, j - fin_fit, c, :]

        def col(name, rows=P):
            return pack[0:rows, COL[name][0]:COL[name][1]]

        tri = pack16[:, F16_TRI:F16_TRI + P]
        ones = pack16[:, F16_ONES:F16_ONES + P]
        iota_lane = pack16[:, F16_IOTA:F16_IOTA + P]
        iota_tile = pack16[:, F16_TILE:F16_TILE + GT]
        ident = col("ident")

        bank = [ctx.enter_context(nc.psum_tensor(f"bank{i}", [P, 512], F32)) for i in range(8)]
        route_ps = bank[0:2]
        pair_ps = bank[2:4]
        cond_ps = bank[4:8]
        x_ps, z_ps, ht_ps, y_ps = bank[4:8]
        out_ps = bank[6:8]

        small_loaded = sem("small_loaded")
        mu_loaded = sem("mu_loaded")
        wdec_loaded = [sem(f"wdec_loaded{i}") for i in range(WG)]
        ut_loaded = sem("ut_loaded")
        x_loaded = [sem(f"x_loaded{c}") for c in range(NC)]
        stage_loaded = [sem(f"stage_loaded{i}") for i in range(STAGE)]
        xrows_loaded = sem("xrows_loaded")
        rows_written = [[sem(f"rows_written{g}{r}") for r in range(2)] for g in range(G)]
        gathered = [sem(f"gathered{r}") for r in range(RING)]
        y_written = [sem(f"y_written{r}") for r in range(RING)]
        edge_written = sem("edge_written")
        fin_loaded = [sem(f"fin_loaded{j}") for j in range(GJ)]
        out_written = sem("out_written")
        decoded = sem("decoded")
        param_done = sem("param_done")
        cond_done = sem("cond_done")
        logits_done = sem("logits_done")
        rows_done = sem("rows_done")
        counts_done = sem("counts_done")
        token_done = sem("token_done")
        sh1_done = sem("sh1_done")
        sh2_done = sem("sh2_done")
        xt_done = sem("xt_done")
        z_done = sem("z_done")
        htr_done = sem("htr_done")
        yps_done = sem("yps_done")
        x_hi = sem("x_hi")
        gate_hi = sem("gate_hi")
        u_copied = sem("u_copied")
        cw_hi = sem("cw_hi")
        w_hi = sem("w_hi")
        o_hi = sem("o_hi")
        rows_copied = sem("rows_copied")
        relu_done = sem("relu_done")
        sh_hi = sem("sh_hi")
        xs_hi = sem("xs_hi")
        ht_hi = sem("ht_hi")
        y_copied = sem("y_copied")
        sigmoid_done = sem("sigmoid_done")
        x_lo = sem("x_lo")
        gate_lo = sem("gate_lo")
        ut_ready = sem("ut_ready")
        cw_lo = sem("cw_lo")
        bias_ready = sem("bias_ready")
        o_ready = sem("o_ready")
        o_lo = sem("o_lo")
        route_step = sem("route_step")
        lg_ready = sem("lg_ready")
        mask_ready = sem("mask_ready")
        onehot_ready = sem("onehot_ready")
        token_ready = sem("token_ready")
        squared = sem("squared")
        sh_lo = sem("sh_lo")
        xs_lo = sem("xs_lo")
        ht_lo = sem("ht_lo")
        acc_ready = sem("acc_ready")
        half_ready = sem("half_ready")
        out_ready = sem("out_ready")
        x_lo_pool = sem("x_lo_pool")
        w_lo = sem("w_lo")

        DVE_X = 3
        GAP = 2
        LAST = NQ - 1
        HEAD = 2 + RING
        LOOPS = (NQ - HEAD - 1) // RING
        TAIL = range(HEAD + RING * LOOPS, NQ)
        BOUNDARY = (GT - 1) // 2
        assert GT % 2 == 1 and 0 < LOOPS and NT % 2 == 0 and GJ * 2 * 256 == NC * KD * CH

        def for_pairs(engine, body):
            for q in range(HEAD):
                body(q, q % RING, q // RING)
            with engine.Fori(0, LOOPS) as i:
                for q0 in range(HEAD, HEAD + RING):
                    body(RING * i + q0, q0 % RING, i + q0 // RING)
            for q in TAIL:
                body(q, q % RING, q // RING)

        def is_first(q):
            return isinstance(q, int) and q == 0

        def is_last(q):
            return isinstance(q, int) and q == LAST

        block = ctx.enter_context(nc.Block())

        @block.sync
        def _(sp):
            sp.dma_start(mu_sb[:, :], mu).then_inc(mu_loaded, 16)
            for n in range(WG):
                g = WG - 1 - n
                lo, hi = g * WK * (D + 1), min((g + 1) * WK, RANK) * (D + 1)
                sp.dma_start(wreg[:, lo:hi], wdec[:, lo:hi]).then_inc(wdec_loaded[n], 16)
                if n == 3:
                    sp.dma_start(pack[:, :], small).then_inc(small_loaded, 16)
                    sp.dma_start(pack16[:, :], small16).then_inc(small_loaded, 16)
            for c in range(NC):
                if c == 2:
                    sp.wait_ge(u_copied, WG)
                sp.dma_start(xo[:, c, :, :], xT[c]).then_inc(x_loaded[c], 16)
            for n in range(E + 1):
                if n < STAGE:
                    first = (N // P * D + (STAGE - 1 - n) * EW) // (WK * (D + 1))
                    sp.wait_ge(decoded, WG - first)
                else:
                    sp.wait_ge(w_hi, n - STAGE + 1)
                    sp.wait_ge(w_lo, n - STAGE + 1)
                e = (n + E) % (E + 1)
                sp.dma_start(stage[n % STAGE], experts[e]).then_inc(stage_loaded[n % STAGE], 16)
                if n == STAGE:
                    sp.wait_ge(decoded, WG)
                    sp.dma_start(acc, xrows_v).then_inc(xrows_loaded, 16)

            def write_y(g, q, r, n, written=None):
                sp.wait_ge(y_copied, n)
                sp.dma_start(y_v[g][bass.ds(q - g * BOUNDARY, 1)].rearrange("a p t d -> p (a t) d"),
                             y_sb[:, r, :, :]).then_inc(y_written[r] if written is None else written, 16)

            def write_all(g, first, end):
                loops = (end - first) // RING
                with sp.Fori(0, loops) as i:
                    for u in range(RING):
                        write_y(g, RING * i + (first + u), (first + u) % RING, RING * i + (first + u + 1))
                for q in range(first + RING * loops, end):
                    write_y(g, q, q % RING, q + 1)

            write_all(0, 0, BOUNDARY)
            write_y(1, BOUNDARY, BOUNDARY % RING, BOUNDARY + 1, edge_written)
            sp.wait_ge(edge_written, 16)
            write_y(0, BOUNDARY, BOUNDARY % RING, BOUNDARY + 1)
            write_all(1, BOUNDARY + 1, NQ)
            for g in range(G):
                for j in range(GJ):
                    sp.wait_ge(out_ready, g * GJ + j + 1)
                    t0 = (g * GJ + j) * P
                    sp.dma_start(out[t0:t0 + P, :], fin(g, j, 1)).then_inc(out_written, 16)
            sp.wait_ge(out_written, 16 * G * GJ)

        @block.gpsimd
        def _(pool):
            for c in range(DVE_X, NC):
                pool.wait_ge(x_hi, c + 1)
                nc.gpsimd.tensor_tensor(xo_lo[:, c, :, :], xo[:, c, :, :], xo_hi[:, c, :, :].bitcast(F32),
                                        ALU.subtract).then_inc(x_lo_pool, 1)
            for n in range(E + 1):
                e = (n + E) % (E + 1)
                pool.wait_ge(w_hi, n + 1)
                nc.gpsimd.tensor_tensor(w_hl[:, e, 1, :], stage[n % STAGE], w_hl[:, e, 0, :].bitcast(F32),
                                        ALU.subtract).then_inc(w_lo, 1)

            def writes(r, pairs):
                return 16 * len(range(r, pairs, RING))

            def gather_y(g, j):
                for c in range(2):
                    nc.gpsimd.indirect_dma_start(
                        out=fin(g, j, c), out_offset=None, in_=y_dram[g],
                        in_offset=bass.IndirectOffsetOnAxis(ap=slot_i[:, g, c, j:j + 1], axis=0),
                    ).then_inc(fin_loaded[j], 16)

            pending = [(0, j) for j in range(GJ)]
            for q in range(NQ):
                for t in range(2):
                    s = 2 * q + t
                    g = s // GT
                    if s == 0:
                        pool.wait_ge(w_lo, E + 1)
                    if s % GT == 0:
                        pool.wait_ge(token_ready, g + 1)
                        for r in range(2):
                            pool.wait_ge(rows_written[g][r], 16 * (GJ // 4))
                    if t == 0 and q >= RING:
                        pool.wait_ge(xt_done, q - RING + 1)
                    nc.gpsimd.indirect_dma_start(
                        out=xs[:, q % RING, t, :], out_offset=None, in_=rows_dram[g],
                        in_offset=bass.IndirectOffsetOnAxis(ap=token_of[:, s:s + 1], axis=0),
                    ).then_inc(gathered[q % RING], 16)
                if q >= BOUNDARY + 6 and pending:
                    if pending[0] == (0, 0):
                        for r in range(RING):
                            pool.wait_ge(y_written[r], writes(r, BOUNDARY + 1))
                        pool.wait_ge(token_done, G)
                        pool.wait_ge(rows_done, G * GJ // 2)
                        pool.wait_ge(o_lo, NC)
                    for _ in range(2):
                        if pending:
                            gather_y(*pending.pop(0))
            while pending:
                gather_y(*pending.pop(0))
            for r in range(RING):
                pool.wait_ge(y_written[r], writes(r, NQ))
            for j in range(GJ):
                gather_y(1, j)

        @block.tensor
        def _(pe):
            mm = nc.tensor.matmul

            def split_product(dst, terms):
                last = None
                for n, ((s_hi, s_lo), (m_hi, m_lo)) in enumerate(terms):
                    mm(dst, s_hi, m_hi, start=(n == 0), stop=False)
                    mm(dst, s_hi, m_lo, start=False, stop=False)
                    last = mm(dst, s_lo, m_hi, start=False, stop=(n == len(terms) - 1))
                return last

            pe.wait_ge(mu_loaded, 16)
            for n in range(WG):
                pe.wait_ge(wdec_loaded[n], 16)
                g = WG - 1 - n
                for j in range(min(WK, RANK - g * WK)):
                    k = g * WK + j
                    last = mm(bank[g][j * LANE:(j + 1) * LANE, 0:D + 1], mu_sb[:, :],
                              wreg[:, k * (D + 1):(k + 1) * (D + 1)], start=True, stop=True)
                last.then_inc(decoded, 1)
            pe.wait_ge(small_loaded, 32)
            pe.wait_ge(ut_ready, 1)
            for b in range(BATCH):
                for h in range(KD):
                    last = mm(pair_ps[b][:, h * D:(h + 1) * D], ut_sb[:, b, h * P:(h + 1) * P], col("V", RANK),
                              start=True, stop=True)
                last.then_inc(param_done, 1)
                if b == 0:
                    for m in range(KD):
                        last = mm(cond_ps[0][:, m * BATCH:(m + 1) * BATCH],
                                  col("V", RANK)[:, m * P:(m + 1) * P], ut_sb[:, :, D], start=True, stop=True)
                    last.then_inc(param_done, 1)

            def cond(c):
                b = c * CH // SEQ
                pe.wait_ge(x_hi, c + 1)
                if c < DVE_X:
                    pe.wait_ge(x_lo, c + 1)
                else:
                    pe.wait_ge(x_lo_pool, c + 1 - DVE_X)
                pe.wait_ge(cw_hi, b + 1)
                pe.wait_ge(cw_lo, b + 1)
                if c == 0:
                    pe.wait_ge(bias_ready, 1)
                for m in range(KD):
                    n = KD * c + m
                    if n >= 4:
                        pe.wait_ge(o_ready, n - 3)
                    terms = [((cw_hl[:, b, 0, k * D + m * P:k * D + (m + 1) * P],
                               cw_hl[:, b, 1, k * D + m * P:k * D + (m + 1) * P]),
                              (xo_hi[:, c, k, :], xo_lo[:, c, k, :])) for k in range(KD)]
                    split_product(cond_ps[n % 4][:, :], terms).then_inc(cond_done, 1)

            def logits(g):
                pe.wait_ge(gate_hi, 1)
                pe.wait_ge(gate_lo, 1)
                for j in range(GJ):
                    c, t = (g * GJ + j) // CT, (g * GJ + j) % CT
                    if t == 0:
                        pe.wait_ge(o_lo, c + 1)
                    n = 0
                    for k in range(KD):
                        for part in (xo_hi, xo_lo):
                            last = mm(route_ps[g][:, j * 2 * E:(j + 1) * 2 * E],
                                      part[:, c, k, t * P:(t + 1) * P],
                                      gate_hl[:, k, :, :].rearrange("p e s -> p (e s)"),
                                      start=(n == 0), stop=(n == 2 * KD - 1))
                            n += 1
                last.then_inc(logits_done, 1)

            def rows(g):
                for n in range(g * GJ // 2, (g + 1) * GJ // 2):
                    if n < 2:
                        pe.wait_ge(cw_lo, n + 1)
                    else:
                        pe.wait_ge(rows_copied, n - 1)
                    for t in range(2):
                        c, tt = (2 * n + t) // CT, (2 * n + t) % CT
                        for k in range(KD):
                            last = nc.tensor.transpose(pair_ps[n % 2][:, t * D + k * P:t * D + (k + 1) * P],
                                                       xo[:, c, k, tt * P:(tt + 1) * P], ident)
                    last.then_inc(rows_done, 1)

            def counts(g):
                pe.wait_ge(mask_ready, g + 1)
                cnt = route_ps[g][:, 0:GJ * E]
                flat = mask16[:, g, :, :].rearrange("p j e -> p (j e)")
                mm(cnt, tri, flat, start=True, stop=False)
                for j in range(GJ - 1):
                    later = GJ - 1 - j
                    mm(route_ps[g][:, (j + 1) * E:GJ * E].rearrange("p (j e) -> p j e", e=E), ones,
                       mask16[:, g, j:j + 1, :].to_broadcast([P, later, E]),
                       start=False, stop=(j == GJ - 2))
                mm(route_ps[g][:, GJ * E:(GJ + 1) * E], ones, msum16[:, g, :],
                   start=True, stop=True).then_inc(counts_done, 1)

            def tokens(g):
                for n in range(2 * GJ):
                    pe.wait_ge(onehot_ready, g * (2 * GJ + 1) + n + 2)
                    last = mm(route_ps[g][:, 0:GT], oh_lane[:, n, :], oh_token[:, n, :],
                              start=(n == 0), stop=(n == 2 * GJ - 1))
                last.then_inc(token_done, 1)

            def w_part(e, part, layer, k, m=None):
                lo = layer * KD * H + k * D
                return w_hl[:, e, part, lo:lo + D] if m is None else w_hl[:, e, part, lo + m * P:lo + (m + 1) * P]

            def shared_first(c):
                if c == 0:
                    pe.wait_ge(w_hi, 1)
                    pe.wait_ge(w_lo, 1)
                pe.wait_ge(o_lo, c + 1)
                for m in range(KD):
                    n = KD * c + m
                    if n < 2:
                        pe.wait_ge(rows_copied, G * GJ // 2)
                    else:
                        pe.wait_ge(squared, (n - 1) if n < KD * GAP + 2 else (n - 1) + NQ)
                    terms = [((w_part(E, 0, 0, k, m), w_part(E, 1, 0, k, m)),
                              (xo_hi[:, c, k, :], xo_lo[:, c, k, :])) for k in range(KD)]
                    split_product(pair_ps[n % 2][:, :], terms).then_inc(sh1_done, 1)

            def shared_second(c):
                pe.wait_ge(sh_hi, KD * (c + 1))
                pe.wait_ge(sh_lo, KD * (c + 1))
                for v in range(2):
                    n = 2 * c + v
                    if n < 2:
                        pe.wait_ge(o_ready, KD * NC)
                    elif n in (2 * GAP, 2 * GAP + 1):
                        pe.wait_ge(ht_lo, NQ)
                        pe.wait_ge(y_copied, NQ)
                    else:
                        pe.wait_ge(acc_ready, n - 1)
                    for t in range(2):
                        at_ = (2 * v + t) * P
                        terms = [((sh_hl[:, 0, k, at_:at_ + P], sh_hl[:, 1, k, at_:at_ + P]),
                                  (w_part(E, 0, 1, k), w_part(E, 1, 1, k))) for k in range(KD)]
                        last = split_product(out_ps[n % 2][:, t * D:(t + 1) * D], terms)
                    last.then_inc(sh2_done, 1)

            for c in range(GC + 1):
                cond(c)
            logits(0)
            for c in range(GC + 1, NC):
                cond(c)
            rows(0)
            counts(0)
            logits(1)
            rows(1)
            shared_first(0)
            tokens(0)
            shared_second(0)
            shared_first(1)
            counts(1)
            shared_second(1)

            def dyn_w(e, part, layer, k):
                lo = layer * KD * H + k * D
                return w_hl[:, bass.ds(e, 1), part, lo:lo + D]

            def transpose_x(r, n_gathered):
                pe.wait_ge(gathered[r], 32 * n_gathered)
                for t in range(2):
                    for k in range(KD):
                        last = nc.tensor.transpose(x_ps[:, (t * KD + k) * P:(t * KD + k + 1) * P],
                                                   xs[:, r, t, k * P:(k + 1) * P], ident)
                last.then_inc(xt_done, 1)

            def first_layer(experts_, q):
                pe.wait_ge(xs_lo, q + 1)
                pe.wait_ge(squared, KD * GAP + q)
                for t in range(2):
                    terms = [((xs_hl[:, 0, t, k, :], xs_hl[:, 1, t, k, :]),
                              (dyn_w(experts_[t], 0, 0, k), dyn_w(experts_[t], 1, 0, k))) for k in range(KD)]
                    last = split_product(z_ps[:, t * H:(t + 1) * H], terms)
                last.then_inc(z_done, 1)

            def second_layer(experts_, q):
                pe.wait_ge(ht_lo, q + 1)
                if not is_first(q):
                    pe.wait_ge(y_copied, q)
                for t in range(2):
                    terms = [((ht_hl[:, 0, t, k, :], ht_hl[:, 1, t, k, :]),
                              (dyn_w(experts_[t], 0, 1, k), dyn_w(experts_[t], 1, 1, k))) for k in range(KD)]
                    last = split_product(y_ps[:, t * D:(t + 1) * D], terms)
                last.then_inc(yps_done, 1)

            def transpose_h(q):
                pe.wait_ge(squared, KD * GAP + q + 1)
                for t in range(2):
                    for k in range(KD):
                        last = nc.tensor.transpose(ht_ps[:, (t * KD + k) * P:(t * KD + k + 1) * P],
                                                   hid[:, t * H + k * P:t * H + (k + 1) * P], ident)
                last.then_inc(htr_done, 1)

            pe.wait_ge(w_lo, E + 1)
            pe.wait_ge(o_ready, KD * NC)
            pe.wait_ge(acc_ready, 2 * GAP)
            transpose_x(0, 1)

            def load_experts(first, pairs):
                regs = owner_regs[0:2 * pairs]
                pe.reg_load(regs, owner[0:1, bass.ds(2 * first, 2 * pairs)])
                values = [pe.snap(r, min_val=0, max_val=E - 1) for r in regs]
                return [values[2 * n:2 * n + 2] for n in range(pairs)]

            def tile_pair(q, slot, turn, now, before):
                first_layer(now, q)
                if not is_last(q):
                    transpose_x((slot + 1) % RING, turn + (slot + 1) // RING + 1)
                if not is_first(q):
                    second_layer(before, q - 1)
                transpose_h(q)

            owner_regs = [pe.alloc_register(f"owner{n}") for n in range(2 * max(HEAD, RING + 1))]
            experts_of = load_experts(0, HEAD)
            for q in range(HEAD):
                tile_pair(q, q % RING, q // RING, experts_of[q], experts_of[q - 1])
                if q == HEAD - 2:
                    tokens(1)
            with pe.Fori(0, LOOPS) as i:
                experts_of = load_experts(RING * i + (HEAD - 1), RING + 1)
                for u in range(RING):
                    q0 = HEAD + u
                    tile_pair(RING * i + q0, q0 % RING, i + q0 // RING, experts_of[u + 1], experts_of[u])
            experts_of = load_experts(TAIL[0] - 1, len(TAIL) + 1)
            for u, q in enumerate(TAIL):
                tile_pair(q, q % RING, q // RING, experts_of[u + 1], experts_of[u])
            second_layer(experts_of[-1], LAST)
            for c in range(GAP, NC):
                shared_first(c)
                shared_second(c)

        @block.scalar
        def _(act):
            copy = nc.scalar.activation

            def split_x(c):
                act.wait_ge(x_loaded[c], 16)
                copy(xo_hi[:, c, :, :], xo[:, c, :, :], ACT.Copy).then_inc(x_hi, 1)

            def split_w(n):
                e = (n + E) % (E + 1)
                act.wait_ge(stage_loaded[n % STAGE], 16 * (n // STAGE + 1))
                copy(w_hl[:, e, 0, :], stage[n % STAGE], ACT.Copy).then_inc(w_hi, 1)

            def split_o(c):
                act.wait_ge(o_ready, KD * (c + 1))
                copy(xo_hi[:, c, :, :], xo[:, c, :, :], ACT.Copy).then_inc(o_hi, 1)

            def copy_rows(n):
                g = 2 * n // GJ
                act.wait_ge(rows_done, n + 1)
                if n >= 2:
                    act.wait_ge(rows_written[2 * (n - 2) // GJ][n % 2], 16 * ((n - 2) % (GJ // 2) // 2 + 1))
                copy(orow[:, n % 2, :, :], pair_ps[n % 2][:, :].rearrange("p (t d) -> p t d", d=D),
                     ACT.Copy).then_inc(rows_copied, 1)
                act.wait_ge(rows_copied, n + 1)
                act.dma_start(rows_v[g][n % (GJ // 2)], orow[:, n % 2, :, :]).then_inc(rows_written[g][n % 2], 16)

            def relu_unit(ps, produced, n_produced, n_squared):
                act.wait_ge(produced, n_produced)
                if n_squared is not None:
                    act.wait_ge(squared, n_squared)
                copy(relu[:, :], ps[:, :], ACT.Relu).then_inc(relu_done, 1)

            def split_shared(c, m, n):
                act.wait_ge(squared, n + 1)
                if c >= 1:
                    act.wait_ge(sh2_done, 2 * c)
                copy(sh_hl[:, 0, m, :], hid[:, :], ACT.Copy).then_inc(sh_hi, 1)

            for n in range(WG):
                g = WG - 1 - n
                rows_ = min(WK, RANK - g * WK) * LANE
                act.wait_ge(decoded, n + 1)
                copy(u_rows[0:rows_, g, :], bank[g][0:rows_, 0:D + 1], ACT.Copy).then_inc(u_copied, 1)
                act.wait_ge(u_copied, n + 1)
                for b in range(BATCH):
                    act.dma_start(ut_sb[g * WK:g * WK + rows_ // LANE, b, :],
                                  u_rows[b:rows_:LANE, g, :]).then_inc(ut_loaded, 16)
            act.wait_ge(small_loaded, 32)
            copy(gate_hl[:, :, :, 0], col("gate").rearrange("p (k e) -> p k e", e=E), ACT.Copy).then_inc(gate_hi, 1)
            for c in range(3):
                split_x(c)
            for b in range(BATCH):
                act.wait_ge(param_done, 2 * b + 1)
                copy(cw_hl[:, b, 0, :], pair_ps[b][:, :], ACT.Copy).then_inc(cw_hi, 1)
            for c in range(3, NC):
                split_x(c)
            split_w(0)
            split_o(0)
            split_w(1)
            split_o(1)
            split_w(2)
            split_o(2)
            split_w(3)
            split_o(3)
            for n in range(GJ // 2):
                copy_rows(n)
            split_w(4)
            for n in range(GJ // 2, GJ):
                copy_rows(n)
            split_w(5)
            act.wait_ge(lg_ready, 1)
            copy(gate_s[:, 0, :], lg[:, 0, :, :].rearrange("p j e -> p (j e)"), ACT.Sigmoid).then_inc(sigmoid_done, 1)
            w_n = 6
            for c in range(GAP):
                for m in range(KD):
                    n = KD * c + m
                    relu_unit(pair_ps[n % 2], sh1_done, n + 1, n if n else None)
                    split_shared(c, m, n)
                    if w_n <= E:
                        split_w(w_n)
                        w_n += 1
            act.wait_ge(lg_ready, 2)
            copy(gate_s[:, 1, :], lg[:, 1, :, :].rearrange("p j e -> p (j e)"), ACT.Sigmoid).then_inc(sigmoid_done, 1)

            def split_xs(q):
                act.wait_ge(xt_done, q + 1)
                if not is_first(q):
                    act.wait_ge(z_done, q)
                copy(xs_hl[:, 0, :, :, :].rearrange("p t k n -> p (t k n)"), x_ps[:, :], ACT.Copy).then_inc(xs_hi, 1)

            def split_ht(q):
                act.wait_ge(htr_done, q + 1)
                if not is_first(q):
                    act.wait_ge(yps_done, q)
                copy(ht_hl[:, 0, :, :, :].rearrange("p t k n -> p (t k n)"), ht_ps[:, :], ACT.Copy).then_inc(ht_hi, 1)

            def copy_y(q, slot, turn):
                act.wait_ge(yps_done, q + 1)
                if not isinstance(turn, int) or turn > 0:
                    act.wait_ge(y_written[slot], 16 * turn)
                copy(y_sb[:, slot, :, :].rearrange("p t d -> p (t d)"), y_ps[:, :], ACT.Copy).then_inc(y_copied, 1)

            UNITS = KD * GAP

            def tile_pair(q, slot, turn):
                relu_unit(z_ps, z_done, q + 1, q + UNITS)
                if not is_last(q):
                    split_xs(q + 1)
                if not is_first(q):
                    copy_y(q - 1, (slot - 1) % RING, turn if slot else turn - 1)
                split_ht(q)

            split_xs(0)
            for_pairs(act, tile_pair)
            copy_y(LAST, LAST % RING, LAST // RING)
            for c in range(GAP, NC):
                for m in range(KD):
                    n = KD * c + m
                    relu_unit(pair_ps[n % 2], sh1_done, n + 1, n + NQ)
                    split_shared(c, m, n + NQ)

        @block.vector
        def _(dve):
            tt, ts, stt, red = (nc.vector.tensor_tensor, nc.vector.tensor_scalar,
                                nc.vector.scalar_tensor_tensor, nc.vector.tensor_reduce)
            steps = [0]

            def step(ins):
                ins.then_inc(route_step, 1)
                steps[0] += 1
                dve.wait_ge(route_step, steps[0])

            def split_x(c):
                dve.wait_ge(x_hi, c + 1)
                tt(xo_lo[:, c, :, :], xo[:, c, :, :], xo_hi[:, c, :, :].bitcast(F32), ALU.subtract).then_inc(x_lo, 1)

            def add_bias(c):
                b = c * CH // SEQ
                for m in range(KD):
                    dve.wait_ge(cond_done, KD * c + KD)
                    ts(xo[:, c, m, :], cond_ps[(KD * c + m) % 4][:, :], bias[:, m, b:b + 1], None,
                       ALU.add).then_inc(o_ready, 1)

            def split_o(c):
                dve.wait_ge(o_hi, c + 1)
                tt(xo_lo[:, c, :, :], xo[:, c, :, :], xo_hi[:, c, :, :].bitcast(F32), ALU.subtract).then_inc(o_lo, 1)

            def choose(g):
                dve.wait_ge(logits_done, g + 1)
                red(lg[:, g, :, :], route_ps[g][:, 0:GJ * 2 * E].rearrange("p (j e s) -> p j e s", e=E, s=2),
                    X_AXIS, ALU.add).then_inc(lg_ready, 1)
                dve.wait_ge(lg_ready, g + 1)
                step(tt(biased[:, 0, :, :], lg[:, g, :, :],
                        col("lb").unsqueeze(1).to_broadcast([P, GJ, E]), ALU.add))
                for c in range(2):
                    step(red(best[:, c, :], biased[:, c, :, :], X_AXIS, ALU.max))
                    step(tt(score[:, :, :], biased[:, c, :, :],
                            best[:, c, :].unsqueeze(2).to_broadcast([P, GJ, E]), ALU.is_equal))
                    step(tt(score[:, :, :], score[:, :, :],
                            col("rank_score").unsqueeze(1).to_broadcast([P, GJ, E]), ALU.mult))
                    step(red(top_score[:, :], score[:, :, :], X_AXIS, ALU.max))
                    step(tt(sel[:, g, c, :, :], score[:, :, :],
                            top_score[:, :].unsqueeze(2).to_broadcast([P, GJ, E]), ALU.is_equal))
                    if c == 0:
                        step(stt(biased[:, 1, :, :], sel[:, g, 0, :, :], -BIG, biased[:, 0, :, :],
                                 ALU.mult, ALU.add))
                step(tt(mask16[:, g, :, :], sel[:, g, 0, :, :], sel[:, g, 1, :, :], ALU.add))
                with nc.allow_low_precision(reason="sums of at most 8 ones are exact in float16"):
                    red(msum16[:, g, :], mask16[:, g, :, :].rearrange("p j e -> p e j"), X_AXIS,
                        ALU.add).then_inc(mask_ready, 1)

            def place_experts(g):
                dve.wait_ge(counts_done, g + 1)
                step(ts(ntile_i[:, :], route_ps[g][:, GJ * E:(GJ + 1) * E], 1.0 / P,
                        (P - 1) / P - (P - 1) / (2 * P), ALU.mult, ALU.add))
                step(nc.vector.tensor_copy(scan[:, 0, 4:], ntile_i[:, :]))
                for n, d in enumerate((1, 2, 4)):
                    step(tt(scan[:, n + 1, 4:], scan[:, n, 4:], scan[:, n, 4 - d:4 + E - d], ALU.add))
                ends = scan[:, 3, 4:]
                step(tt(scan[:, 1, 4:], ends, scan[:, 0, 4:], ALU.subtract))

            def place_slots(g):
                step(stt(slot_e[:, :, :], scan[:, 1, 4:].unsqueeze(1).to_broadcast([P, GJ, E]), float(P),
                         route_ps[g][:, 0:GJ * E].rearrange("p (j e) -> p j e", e=E), ALU.mult, ALU.add))
                step(tt(picked[:, :, :, :].rearrange("p c j e -> p c (j e)"),
                        sel[:, g, :, :, :].rearrange("p c j e -> p c (j e)"),
                        slot_e[:, :, :].rearrange("p j e -> p (j e)").unsqueeze(1).to_broadcast([P, 2, GJ * E]),
                        ALU.mult))
                step(red(slot[:, :, :], picked[:, :, :, :], X_AXIS, ALU.add))
                step(ts(tile_i[:, :, :], slot[:, :, :], 1.0 / P, -(P - 1) / (2 * P), ALU.mult, ALU.add))
                step(nc.vector.tensor_copy(tile_f[:, :, :], tile_i[:, :, :]))
                step(stt(lane_f[:, :, :], tile_f[:, :, :], -float(P), slot[:, :, :], ALU.mult, ALU.add))

            def one_hot_tiles(g):
                if g:
                    dve.wait_ge(token_done, g)
                step(tt(oh_tile[:, :, :], iota_tile.unsqueeze(1).to_broadcast([P, 2 * GJ, GT]),
                        tile_f[:, :, :].rearrange("p c j -> p (c j)").unsqueeze(2).to_broadcast([P, 2 * GJ, GT]),
                        ALU.is_equal))
                token = col("token")
                tt(oh_token[:, :, :].rearrange("p (c j) n -> p c j n", c=2),
                   oh_tile[:, :, :].rearrange("p (c j) n -> p c j n", c=2),
                   token.unsqueeze(1).unsqueeze(3).to_broadcast([P, 2, GJ, GT]), ALU.mult).then_inc(onehot_ready, 1)

            def one_hot_lanes(first, end):
                for n in range(first, end):
                    ts(oh_lane[:, n, :], iota_lane, lane_f[:, n // GJ, n % GJ:n % GJ + 1], None,
                       ALU.is_equal).then_inc(onehot_ready, 1)

            def owners(g):
                step(tt(owner_cmp[:, :, :],
                        pack[0:1, COL["tile_no"][0]:COL["tile_no"][1]].unsqueeze(2).to_broadcast([1, GT, E]),
                        scan[0:1, 3, 4:].unsqueeze(1).to_broadcast([1, GT, E]), ALU.is_ge))
                step(red(owner_f[:, :], owner_cmp[:, :, :], X_AXIS, ALU.add))
                step(ts(owner[:, g * GT:(g + 1) * GT], owner_f[:, :], float(E - 1), None, ALU.min))
                step(ts(slot_i[:, g, :, :], slot[:, :, :], float(g * P), None, ALU.add))

            def token_ids(g):
                dve.wait_ge(token_done, g + 1)
                nc.vector.tensor_copy(token_of[:, g * GT:(g + 1) * GT], route_ps[g][:, 0:GT]).then_inc(token_ready, 1)

            def weights(g):
                dve.wait_ge(sigmoid_done, g + 1)
                step(tt(picked[:, :, :, :].rearrange("p c j e -> p c (j e)"),
                        sel[:, g, :, :, :].rearrange("p c j e -> p c (j e)"),
                        gate_s[:, g, :].unsqueeze(1).to_broadcast([P, 2, GJ * E]), ALU.mult))
                step(red(wgt[:, g, :, :], picked[:, :, :, :], X_AXIS, ALU.add))
                step(tt(wsum[:, :], wgt[:, g, 0, :], wgt[:, g, 1, :], ALU.add))
                step(ts(wsum[:, :], wsum[:, :], 1e-6, None, ALU.add))
                step(nc.vector.reciprocal(wsum[:, :], wsum[:, :]))
                step(tt(wgt[:, g, :, :], wgt[:, g, :, :], wsum[:, :].unsqueeze(1).to_broadcast([P, 2, GJ]), ALU.mult))

            def square(ps, n, n_free, free):
                dve.wait_ge(relu_done, n + 1)
                if free is not None:
                    dve.wait_ge(free, n_free)
                stt(hid[:, :], ps[:, :], 0.0, relu[:, :], ALU.max, ALU.mult).then_inc(squared, 1)

            def shared_unit(c, m, n, n_free, free):
                square(pair_ps[(KD * c + m) % 2], n, n_free, free)
                dve.wait_ge(sh_hi, KD * c + m + 1)
                tt(sh_hl[:, 1, m, :], hid[:, :], sh_hl[:, 0, m, :].bitcast(F32), ALU.subtract).then_inc(sh_lo, 1)

            def add_shared(n):
                dve.wait_ge(xrows_loaded, 16)
                dve.wait_ge(sh2_done, n + 1)
                tt(acc[:, 2 * n:2 * n + 2, :], out_ps[n % 2][:, :].rearrange("p (t d) -> p t d", d=D),
                   acc[:, 2 * n:2 * n + 2, :], ALU.add).then_inc(acc_ready, 1)

            dve.wait_ge(small_loaded, 32)
            step(nc.vector.memset(scan[:, :, :], 0.0))
            dve.wait_ge(ut_loaded, 16 * WG * BATCH)
            tt(ut_sb[:, :, :], ut_sb[:, :, :], col("b_dec", RANK).unsqueeze(1).to_broadcast([RANK, BATCH, D + 1]),
               ALU.add).then_inc(ut_ready, 1)
            dve.wait_ge(gate_hi, 1)
            tt(gate_hl[:, :, :, 1], col("gate").rearrange("p (k e) -> p k e", e=E),
               gate_hl[:, :, :, 0].bitcast(F32), ALU.subtract).then_inc(gate_lo, 1)
            for c in range(2):
                split_x(c)
            for b in range(BATCH):
                dve.wait_ge(cw_hi, b + 1)
                tt(cw_hl[:, b, 1, :], pair_ps[b][:, :], cw_hl[:, b, 0, :].bitcast(F32), ALU.subtract)\
                    .then_inc(cw_lo, 1)
                if b == 0:
                    dve.wait_ge(param_done, 2)
                    nc.vector.tensor_copy(bias[:, :, :],
                                          cond_ps[0][:, 0:KD * BATCH].rearrange("p (m b) -> p m b", b=BATCH))\
                        .then_inc(bias_ready, 1)
            for c in range(2, DVE_X):
                split_x(c)
            dve.wait_ge(bias_ready, 1)
            for c in range(GC + 1):
                add_bias(c)
                split_o(c)
            choose(0)
            for c in range(GC + 1, NC):
                add_bias(c)
                split_o(c)
            place_experts(0)
            place_slots(0)
            one_hot_tiles(0)
            one_hot_lanes(0, 2 * GJ)
            owners(0)
            token_ids(0)
            UNITS = KD * GAP
            for m in range(KD):
                shared_unit(0, m, m, m, sh_lo if m else None)
            choose(1)
            for m in range(KD):
                shared_unit(1, m, KD + m, KD + m, sh_lo)
            for n in range(2 * GAP):
                add_shared(n)

            def route_beside(q, place):
                if place == 0:
                    if q == 0:
                        place_experts(1)
                    if q == 1:
                        one_hot_tiles(1)
                    if q in (2, 3):
                        one_hot_lanes(4 * (2 * q - 3), 4 * (2 * q - 2))
                    if q == 4:
                        weights(0)
                if place == 1:
                    if q == 0:
                        place_slots(1)
                    if q in (1, 2):
                        one_hot_lanes(8 * (q - 1), 8 * (q - 1) + 4)
                    if q == 3:
                        owners(1)
                    if q == 4:
                        token_ids(1)
                        weights(1)

            def split_xs(q):
                dve.wait_ge(xs_hi, q)
                tt(xs_hl[:, 1, :, :, :].rearrange("p t k n -> p (t k n)"), x_ps[:, :],
                   xs_hl[:, 0, :, :, :].rearrange("p t k n -> p (t k n)").bitcast(F32), ALU.subtract)\
                    .then_inc(xs_lo, 1)

            def split_ht(q):
                dve.wait_ge(ht_hi, q)
                tt(ht_hl[:, 1, :, :, :].rearrange("p t k n -> p (t k n)"), ht_ps[:, :],
                   ht_hl[:, 0, :, :, :].rearrange("p t k n -> p (t k n)").bitcast(F32), ALU.subtract)\
                    .then_inc(ht_lo, 1)

            def tile_pair(q, slot, turn):
                if is_first(q):
                    square(z_ps, UNITS, UNITS, sh_lo)
                else:
                    square(z_ps, q + UNITS, q, htr_done)
                if not is_last(q):
                    split_xs(q + 2)
                if isinstance(q, int) and q < HEAD:
                    route_beside(q, 0)
                split_ht(q + 1)
                if isinstance(q, int) and q < HEAD:
                    route_beside(q, 1)

            split_xs(1)
            for_pairs(dve, tile_pair)

            def combine(g, j):
                dve.wait_ge(fin_loaded[j], 32 * (g + 1))
                stt(fin(g, j, 0), fin(g, j, 0), wgt[:, g, 0, j:j + 1], acc[:, g * GJ + j, :],
                    ALU.mult, ALU.add).then_inc(half_ready, 1)
                dve.wait_ge(half_ready, g * GJ + j + 1)
                stt(fin(g, j, 1), fin(g, j, 1), wgt[:, g, 1, j:j + 1], fin(g, j, 0),
                    ALU.mult, ALU.add).then_inc(out_ready, 1)

            done = 0
            for c in range(GAP, NC):
                for m in range(KD):
                    n = KD * c + m
                    shared_unit(c, m, n + NQ, NQ if n == UNITS else n, htr_done if n == UNITS else sh_lo)
                    for _ in range(GJ // (KD * (NC - GAP))):
                        combine(0, done)
                        done += 1
                add_shared(2 * c)
                add_shared(2 * c + 1)
            for j in range(GJ):
                if j % 2 == 0:
                    dve.wait_ge(acc_ready, GJ // 2 + j // 2 + 1)
                combine(1, j)


def kernel(x, cond_512, L0_cond_W_dec, L0_cond_b_dec, L0_cond_V, L0_ffn_gate_w, L0_ffn_lb_bias,
           L0_ffn_w1, L0_ffn_w2, L0_ffn_cfc, L0_ffn_cproj):
    import numpy as np
    import concourse.bacc as bacc
    from concourse.bass_utils import run_bass_kernel_spmd

    def arr(a):
        return np.asarray(a)

    rows = arr(x).reshape(N, D)
    x_t = np.ascontiguousarray(rows.T.reshape(KD, P, NC, CH).transpose(2, 1, 0, 3))
    wdec = np.ascontiguousarray(arr(L0_cond_W_dec).reshape(MU, D + 1, RANK).transpose(0, 2, 1)).reshape(MU, -1)
    b_dec = arr(L0_cond_b_dec).reshape(D + 1, RANK)

    mu = np.zeros((P, LANE), np.float32)
    mu[:, 0:BATCH] = arr(cond_512).T
    small = np.zeros((P, PACK), np.float32)

    def put(name, a):
        small[0:a.shape[0], COL[name][0]:COL[name][1]] = a

    put("b_dec", b_dec.T)
    put("gate", arr(L0_ffn_gate_w).T.reshape(KD, P, E).transpose(1, 0, 2).reshape(P, -1))
    put("lb", np.tile(arr(L0_ffn_lb_bias), (P, 1)))
    put("V", arr(L0_cond_V))
    put("rank_score", np.tile(np.arange(E, 0, -1, dtype=np.float32), (P, 1)))
    put("token", (np.arange(GJ)[None, :] * P + np.arange(P)[:, None]).astype(np.float32))
    put("tile_no", np.tile(np.arange(GT, dtype=np.float32), (P, 1)))
    put("ident", np.eye(P, dtype=np.float32))
    small16 = np.zeros((P, F16_PACK), np.float16)
    small16[:, F16_TRI:F16_TRI + P] = np.triu(np.ones((P, P), np.float16), 1)
    small16[:, F16_ONES:F16_ONES + P] = 1
    small16[:, F16_IOTA:F16_IOTA + P] = np.arange(P)
    small16[:, F16_TILE:F16_TILE + GT] = np.arange(GT)

    def halves(w):
        return w.T.reshape(KD, P, -1).transpose(1, 0, 2).reshape(P, -1)

    first = [arr(L0_ffn_w1)[e] for e in range(E)] + [arr(L0_ffn_cfc)]
    second = [arr(L0_ffn_w2)[e] for e in range(E)] + [arr(L0_ffn_cproj)]
    experts = np.stack([np.concatenate([halves(a), halves(b)], axis=1) for a, b in zip(first, second)])

    arrays = {"mu_dram": mu, "small_dram": small, "small16_dram": small16, "wdec_dram": wdec, "xT_dram": x_t,
              "xrows_dram": np.ascontiguousarray(rows), "experts_dram": np.ascontiguousarray(experts)}
    nc = bacc.Bacc("TRN2", target_bir_lowering=False, num_devices=1)
    args = [nc.dram_tensor(k, a.shape, mybir.dt.from_np(a.dtype), kind="ExternalInput").ap()
            for k, a in arrays.items()]
    out = nc.dram_tensor("out_dram", (N, D), F32, kind="ExternalOutput").ap()
    build_moe(nc, *args, out)
    r = run_bass_kernel_spmd(nc, [arrays], core_ids=[0])
    return r.results[0]["out_dram"].reshape(BATCH, SEQ, D)
```

```python
from contextlib import ExitStack

import concourse.bass as bass
from concourse import mybir

F32 = mybir.dt.float32
F32R = mybir.dt.float32r
F16 = mybir.dt.float16
I32 = mybir.dt.int32
ALU = mybir.AluOpType
ACT = mybir.ActivationFunctionType
X_AXIS = mybir.AxisListType.X

P = 128
BATCH, SEQ, D = 2, 1024, 256
N = BATCH * SEQ
E, H = 8, 256
MU, RANK = 128, 30
KD = D // P
CH = 512
NC = N // CH
CT = CH // P
G = 2
GN = N // G
GJ = GN // P
GC = NC // G
GT = (2 * GN + E * (P - 1)) // P
NT = G * GT
NQ = NT // 2
RING = 3
LANE = 32
WK = 4
WG = -(-RANK // WK)
MUZ = 2 * LANE - 1
ORING = 4
GAP = 1
TURN = 2 * RING
EW = KD * H + KD * D
BIG = 3.0e38

_WIDTHS = [("gate", KD * E), ("lb", E), ("rank_score", E), ("token", GJ), ("tile_no", GT),
           ("b_dec", D + 1), ("ident", P), ("V", BATCH * D)]
COL, _at = {}, 0
for _name, _width in _WIDTHS:
    COL[_name] = (_at, _at + _width)
    _at += _width
PACK = _at
F16_TRI, F16_ONES, F16_IOTA, F16_TILE, F16_PACK = 0, P, 2 * P, 3 * P, 3 * P + GT + GT % 2


def build_moe(nc, mu, small, small16, wdec, xT, xrows, experts, out):
    rows_dram = [nc.dram_tensor(f"cond_rows{g}", (GN, D), F32, kind="Internal").ap() for g in range(G)]
    y_dram = [nc.dram_tensor(f"expert_rows{g}", ((GT + 1) * P, D), F32, kind="Internal").ap() for g in range(G)]
    rows_v = [a.rearrange("(n t p) d -> n p t d", t=2, p=P) for a in rows_dram]
    y_v = [a.rearrange("(n t p) d -> n p t d", t=2, p=P) for a in y_dram]
    xrows_v = xrows.rearrange("(j p) d -> p j d", p=P)

    with ExitStack() as ctx:
        def sb(name, shape, dt=F32):
            return ctx.enter_context(nc.sbuf_tensor(name, shape, dt))

        def sem(name):
            return ctx.enter_context(nc.semaphore(name))

        mu_sb = sb("mu_sb", [P, BATCH * MUZ])
        pack = sb("pack", [P, PACK])
        pack16 = sb("pack16", [P, F16_PACK], F16)
        wreg = sb("wdec_region", [P, RANK * (D + 1)])
        xo = sb("x_then_o", [P, NC, KD, CH])
        xo_hi = sb("xo_hi", [P, NC, KD, CH], F32R)
        xo_lo = sb("xo_lo", [P, NC, KD, CH], F32R)
        w_hl = sb("w_hl", [P, E + 1, 2, EW], F32R)
        cw_hl = sb("cw_hl", [P, BATCH, 2, KD * D], F32R)
        gate_hl = sb("gate_hl", [P, KD, E, 2], F32R)
        ut_sb = sb("ut_sb", [P, D + 1])
        bias = sb("bias", [P, KD, BATCH])
        scratch = sb("scratch", [P, ORING * 2 * D])
        orow = scratch[:, :].rearrange("p (s t d) -> p s t d", s=ORING, t=2)
        relus = [scratch[:, n * 4 * H:n * 4 * H + 2 * H] for n in range(2)]
        hids = [scratch[:, n * 4 * H + 2 * H:(n + 1) * 4 * H] for n in range(2)]
        hid = hids[0]
        FRONT = 2
        pair_hl = sb("pair_hl", [P, 2, 2, 2, KD, P], F32R)
        xs_hl, ht_hl = pair_hl[:, 0], pair_hl[:, 1]
        sh_own = sb("sh_hl", [P, 2, KD, CH], F32R)
        sh_pair = pair_hl[:, :, :, :, :, :].rearrange("p a h t k n -> p a h (t k n)")

        def sh_hl(c):
            return sh_pair if c >= GAP and (c - GAP) % 2 else sh_own

        lg = sb("logits", [P, G, GJ, E])
        biased = sb("biased", [P, 2, GJ, E])
        best = sb("best", [P, 2, GJ])
        score = sb("score", [P, GJ, E])
        top_score = sb("top_score", [P, GJ])
        sel = sb("sel", [P, G, 2, GJ, E])
        mask16 = sb("mask16", [P, G, GJ, E], F16)
        msum16 = sb("msum16", [P, G, E], F16)
        ntile_i = sb("ntile_i", [P, E], I32)
        scan = sb("scan", [P, 4, 4 + E])
        slot_e = sb("slot_e", [P, GJ, E])
        picked = sb("picked", [P, 2, GJ, E])
        slot = sb("slot", [P, 2, GJ])
        tile_i = sb("tile_i", [P, 2, GJ], I32)
        tile_f = sb("tile_f", [P, 2, GJ])
        lane_f = sb("lane_f", [P, 2, GJ])
        oh_tile = sb("oh_tile", [P, 2 * GJ, GT], F16)
        oh_token = sb("oh_token", [P, 2 * GJ, GT], F16)
        oh_lane = sb("oh_lane", [P, 2 * GJ, P], F16)
        owner_cmp = sb("owner_cmp", [1, GT, E])
        owner_f = sb("owner_f", [1, GT])
        owner = sb("owner", [1, NT + 2 * TURN], I32)
        token_of = sb("token_of", [P, NT], I32)
        slot_i = sb("slot_i", [P, G, 2, GJ], I32)
        gate_s = sb("gate_s", [P, G, GJ * E])
        gate_of = sb("gate_of", [P, G, 2, GJ, E])
        wsum = sb("wsum", [P, G, GJ])
        wgt = sb("wgt", [P, G, 2, GJ])

        acc = wreg[:, 0:N // P * D].rearrange("p (j d) -> p j d", d=D)
        at = N // P * D
        xs = wreg[:, at:at + RING * 2 * D].rearrange("p (r t d) -> p r t d", r=RING, t=2)
        at += RING * 2 * D
        y_sb = wreg[:, at:at + RING * 2 * D].rearrange("p (r t d) -> p r t d", r=RING, t=2)
        relus.append(y_sb[:, 1, :, :].rearrange("p t d -> p (t d)"))
        hids.append(y_sb[:, 2, :, :].rearrange("p t d -> p (t d)"))
        STAGE = (at + RING * 2 * D - N // P * D) // EW
        stage = [wreg[:, N // P * D + (STAGE - 1 - n) * EW:N // P * D + (STAGE - n) * EW] for n in range(STAGE)]
        fin_xo = xo[:, :, :, :].rearrange("p c k n -> p (c k n)")
        fin_at = N // P * D
        fin_fit = (RANK * (D + 1) - fin_at) // (2 * D)

        def fin(g, j, c):
            if g == 0:
                return fin_xo[:, (2 * j + c) * D:(2 * j + c + 1) * D]
            if j < fin_fit:
                return wreg[:, fin_at + (2 * j + c) * D:fin_at + (2 * j + c + 1) * D]
            return orow[:, ORING - 2 + j - fin_fit, c, :]

        def fins(g, j, n, c):
            base, at_ = (fin_xo, 0) if g == 0 else (wreg, fin_at)
            if g == 1 and j >= fin_fit:
                return fin(g, j, c).unsqueeze(1)
            return base[:, at_ + 2 * j * D:at_ + 2 * (j + n) * D]\
                .rearrange("p (j c d) -> p j c d", c=2, d=D)[:, :, c, :]

        def col(name, rows=P):
            return pack[0:rows, COL[name][0]:COL[name][1]]

        tri = pack16[:, F16_TRI:F16_TRI + P]
        ones = pack16[:, F16_ONES:F16_ONES + P]
        iota_lane = pack16[:, F16_IOTA:F16_IOTA + P]
        iota_tile = pack16[:, F16_TILE:F16_TILE + GT]
        ident = col("ident")

        bank = [ctx.enter_context(nc.psum_tensor(f"bank{i}", [P, 512], F32)) for i in range(8)]
        route_ps = bank[0:2]
        pair_ps = bank[2:4]
        cond_ps = bank[4:8]
        x_ps, z_ps, ht_ps, y_ps = bank[4:8]
        out_ps = bank[6:8]

        def first_ps(c, m):
            return pair_ps[m] if c % 2 else bank[4 + m]

        small_loaded = sem("small_loaded")
        mu_loaded = sem("mu_loaded")
        wdec_loaded = [sem(f"wdec_loaded{i}") for i in range(WG)]
        x_loaded = [sem(f"x_loaded{c}") for c in range(NC)]
        stage_loaded = [sem(f"stage_loaded{i}") for i in range(STAGE)]
        xrows_loaded = [sem(f"xrows_loaded{i}") for i in range(2)]
        rows_written = [[sem(f"rows_written{g}{r}") for r in range(ORING)] for g in range(G)]
        gathered = [sem(f"gathered{r}") for r in range(RING)]
        y_written = [sem(f"y_written{r}") for r in range(RING)]
        edge_written = sem("edge_written")
        fin_loaded = [[sem(f"fin_loaded{g}{j}") for j in range(GJ)] for g in range(G)]
        out_written = sem("out_written")
        decoded = sem("decoded")
        param_done = sem("param_done")
        cond_done = sem("cond_done")
        logits_done = sem("logits_done")
        rows_done = sem("rows_done")
        counts_done = sem("counts_done")
        token_done = sem("token_done")
        sh1_done = sem("sh1_done")
        sh2_done = sem("sh2_done")
        xt_done = sem("xt_done")
        z_done = sem("z_done")
        htr_done = sem("htr_done")
        yps_done = sem("yps_done")
        x_hi = sem("x_hi")
        gate_hi = sem("gate_hi")
        cw_hi = sem("cw_hi")
        w_hi = sem("w_hi")
        o_top = sem("o_top")
        o_hi = sem("o_hi")
        rows_copied = sem("rows_copied")
        relu_done = sem("relu_done")
        sh_hi = sem("sh_hi")
        xs_hi = sem("xs_hi")
        ht_hi = sem("ht_hi")
        y_copied = sem("y_copied")
        sigmoid_done = sem("sigmoid_done")
        weighted = sem("weighted")
        x_lo = sem("x_lo")
        gate_lo = sem("gate_lo")
        ut_ready = sem("ut_ready")
        cw_lo = sem("cw_lo")
        bias_ready = sem("bias_ready")
        o_bottom = sem("o_bottom")
        o_lo = sem("o_lo")
        route_step = sem("route_step")
        lg_ready = sem("lg_ready")
        mask_ready = sem("mask_ready")
        onehot_ready = sem("onehot_ready")
        token_ready = sem("token_ready")
        owners_ready = sem("owners_ready")
        squared = sem("squared")
        sh_lo = sem("sh_lo")
        xs_lo = sem("xs_lo")
        ht_lo = sem("ht_lo")
        acc_ready = sem("acc_ready")
        weights_ready = sem("weights_ready")
        half_ready = sem("half_ready")
        w_lo_dve = sem("w_lo_dve")
        out_ready = sem("out_ready")
        x_lo_pool = sem("x_lo_pool")
        w_lo = sem("w_lo")

        DVE_W = (2, 8)
        DVE_X = 3
        LAST = NQ - 1
        COUNTS_AT, TOKENS_AT = 0, 7
        HEAD = 2 + 2 * RING
        LOOPS = (NQ - HEAD - 1) // TURN
        TAIL = range(HEAD + TURN * LOOPS, NQ)
        BOUNDARY = (GT - 1) // 2
        assert GAP == 1 and GT % 2 == 1 and NT % 2 == 0 and 0 < len(TAIL) <= TURN and 0 < LOOPS
        assert GJ * 2 * D == NC * KD * CH

        def wait_w_lo(engine, n):
            by_dve = len([m for m in DVE_W if m <= n])
            engine.wait_ge(w_lo, n + 1 - by_dve)
            if by_dve:
                engine.wait_ge(w_lo_dve, by_dve)

        def for_pairs(engine, body):
            for q in range(HEAD):
                body(q, q % RING, q // RING)
            with engine.Fori(0, LOOPS) as i:
                for q0 in range(HEAD, HEAD + TURN):
                    body(TURN * i + q0, q0 % RING, TURN // RING * i + q0 // RING)
            for q in TAIL:
                body(q, q % RING, q // RING)

        def is_first(q):
            return isinstance(q, int) and q == 0

        def is_last(q):
            return isinstance(q, int) and q == LAST

        block = ctx.enter_context(nc.Block())

        @block.sync
        def _(sp):
            sp.dma_start(mu_sb[:, :], mu).then_inc(mu_loaded, 16)
            for n in range(WG):
                g = WG - 1 - n
                lo, hi = g * WK * (D + 1), min((g + 1) * WK, RANK) * (D + 1)
                sp.dma_start(wreg[:, lo:hi], wdec[:, lo:hi]).then_inc(wdec_loaded[n], 16)
                if n == 3:
                    sp.dma_start(pack[:, :], small).then_inc(small_loaded, 16)
                    sp.dma_start(pack16[:, :], small16).then_inc(small_loaded, 16)
            for c in range(NC):
                sp.dma_start(xo[:, c, :, :], xT[c]).then_inc(x_loaded[c], 16)
            for n in range(E + 1):
                if n < STAGE:
                    first = (N // P * D + (STAGE - 1 - n) * EW) // (WK * (D + 1))
                    sp.wait_ge(decoded, WG - first)
                else:
                    sp.wait_ge(w_hi, n - STAGE + 1)
                    wait_w_lo(sp, n - STAGE)
                e = (n + E) % (E + 1)
                sp.dma_start(stage[n % STAGE], experts[e]).then_inc(stage_loaded[n % STAGE], 16)
            sp.wait_ge(decoded, WG)
            sp.dma_start(acc[:, 0:CT * GAP, :], xrows_v[:, 0:CT * GAP, :]).then_inc(xrows_loaded[0], 16)
            sp.wait_ge(xt_done, RING)
            sp.dma_start(acc[:, CT * GAP:, :], xrows_v[:, CT * GAP:, :]).then_inc(xrows_loaded[1], 16)

            def write_y(g, q, r, n, written=None):
                sp.wait_ge(y_copied, n)
                sp.dma_start(y_v[g][bass.ds(q - g * BOUNDARY, 1)].rearrange("a p t d -> p (a t) d"),
                             y_sb[:, r, :, :]).then_inc(y_written[r] if written is None else written, 16)

            def write_all(g, first, end):
                loops = (end - first) // RING
                with sp.Fori(0, loops) as i:
                    for u in range(RING):
                        write_y(g, RING * i + (first + u), (first + u) % RING, RING * i + (first + u + 1))
                for q in range(first + RING * loops, end):
                    write_y(g, q, q % RING, q + 1)

            write_all(0, 0, BOUNDARY)
            write_y(1, BOUNDARY, BOUNDARY % RING, BOUNDARY + 1, edge_written)
            sp.wait_ge(edge_written, 16)
            write_y(0, BOUNDARY, BOUNDARY % RING, BOUNDARY + 1)
            write_all(1, BOUNDARY + 1, NQ)
            for g in range(G):
                for j in range(GJ):
                    sp.wait_ge(out_ready, g * GJ + j + 1)
                    t0 = (g * GJ + j) * P
                    sp.dma_start(out[t0:t0 + P, :], fin(g, j, 1)).then_inc(out_written, 16)
            sp.wait_ge(out_written, 16 * G * GJ)

        @block.gpsimd
        def _(pool):
            for c in range(DVE_X, NC):
                pool.wait_ge(x_hi, c + 1)
                nc.gpsimd.tensor_tensor(xo_lo[:, c, :, :], xo[:, c, :, :], xo_hi[:, c, :, :].bitcast(F32),
                                        ALU.subtract).then_inc(x_lo_pool, 1)
            for n in range(E + 1):
                if n in DVE_W:
                    continue
                e = (n + E) % (E + 1)
                pool.wait_ge(w_hi, n + 1)
                nc.gpsimd.tensor_tensor(w_hl[:, e, 1, :], stage[n % STAGE], w_hl[:, e, 0, :].bitcast(F32),
                                        ALU.subtract).then_inc(w_lo, 1)

            def writes(r, pairs):
                return 16 * len(range(r, pairs, RING))

            def gather_y(g, j, c):
                if (g, j, c) == (0, 0, 0):
                    for r in range(RING):
                        pool.wait_ge(y_written[r], writes(r, BOUNDARY + 1))
                    pool.wait_ge(token_done, G)
                    pool.wait_ge(rows_done, G * GJ // 2)
                    pool.wait_ge(o_lo, NC)
                nc.gpsimd.indirect_dma_start(
                    out=fin(g, j, c), out_offset=None, in_=y_dram[g],
                    in_offset=bass.IndirectOffsetOnAxis(ap=slot_i[:, g, c, j:j + 1], axis=0),
                ).then_inc(fin_loaded[g][j], 16)

            pending = [(0, j, c) for j in range(GJ) for c in range(2)]
            for q in range(NQ):
                for t in range(2):
                    s = 2 * q + t
                    g = s // GT
                    if s == 0:
                        wait_w_lo(pool, E)
                    if s % GT == 0:
                        pool.wait_ge(token_ready, g + 1)
                        for r in range(ORING):
                            pool.wait_ge(rows_written[g][r], 16 * (GJ // (2 * ORING)))
                    if t == 0 and q >= RING:
                        pool.wait_ge(xt_done, q - RING + 1)
                    nc.gpsimd.indirect_dma_start(
                        out=xs[:, q % RING, t, :], out_offset=None, in_=rows_dram[g],
                        in_offset=bass.IndirectOffsetOnAxis(ap=token_of[:, s:s + 1], axis=0),
                    ).then_inc(gathered[q % RING], 16)
                if q >= BOUNDARY + 5:
                    gather_y(*pending.pop(0))
            for g, j, c in pending:
                gather_y(g, j, c)
            for r in range(RING):
                pool.wait_ge(y_written[r], writes(r, NQ))
            for j in range(GJ):
                if j == fin_fit:
                    pool.wait_ge(squared, NQ + KD * NC)
                for c in range(2):
                    gather_y(1, j, c)

        @block.tensor
        def _(pe):
            mm = nc.tensor.matmul

            def split_product(dst, terms):
                last = None
                for n, ((s_hi, s_lo), (m_hi, m_lo)) in enumerate(terms):
                    mm(dst, s_hi, m_hi, start=(n == 0), stop=False)
                    mm(dst, s_hi, m_lo, start=False, stop=False)
                    last = mm(dst, s_lo, m_hi, start=False, stop=(n == len(terms) - 1))
                return last

            pe.wait_ge(mu_loaded, 16)
            for n in range(WG):
                pe.wait_ge(wdec_loaded[n], 16)
                g = WG - 1 - n
                ranks = range(g * WK, min((g + 1) * WK, RANK))
                for k in reversed(ranks):
                    for b in range(BATCH):
                        tile = k % 2 * BATCH + b
                        at_ = b * MUZ + LANE - 1 - k
                        last = mm(route_ps[0][tile * LANE:(tile + 1) * LANE, 0:D + 1], mu_sb[:, at_:at_ + LANE],
                                  wreg[:, k * (D + 1):(k + 1) * (D + 1)],
                                  start=(k >= RANK - 2), stop=(k < 2))
                last.then_inc(decoded, 1)
            pe.wait_ge(small_loaded, 32)
            pe.wait_ge(ut_ready, 1)
            v_of = [col("V")[:, b * D:(b + 1) * D] for b in range(BATCH)]
            for b in range(BATCH):
                for h in range(KD):
                    last = mm(pair_ps[b][:, h * D:(h + 1) * D], ut_sb[:, h * P:(h + 1) * P], v_of[b],
                              start=True, stop=True)
                last.then_inc(param_done, 1)
            for m in range(KD):
                for b in range(BATCH):
                    last = mm(cond_ps[3][:, m * BATCH + b:m * BATCH + b + 1], v_of[b][:, m * P:(m + 1) * P],
                              ut_sb[:, D:D + 1], start=True, stop=True)
            last.then_inc(param_done, 1)

            def cond(c):
                b = c * CH // SEQ
                pe.wait_ge(x_hi, c + 1)
                if c < DVE_X:
                    pe.wait_ge(x_lo, c + 1)
                else:
                    pe.wait_ge(x_lo_pool, c + 1 - DVE_X)
                pe.wait_ge(cw_hi, b + 1)
                pe.wait_ge(cw_lo, b + 1)
                for m in range(KD):
                    n = KD * c + m
                    if n == 3:
                        pe.wait_ge(bias_ready, 1)
                    if n >= 4:
                        pe.wait_ge([o_bottom, o_top][m], c - 1)
                    terms = [((cw_hl[:, b, 0, k * D + m * P:k * D + (m + 1) * P],
                               cw_hl[:, b, 1, k * D + m * P:k * D + (m + 1) * P]),
                              (xo_hi[:, c, k, :], xo_lo[:, c, k, :])) for k in range(KD)]
                    split_product(cond_ps[n % 4][:, :], terms).then_inc(cond_done, 1)

            def logits(c):
                g = c // GC
                pe.wait_ge(gate_hi, 1)
                pe.wait_ge(gate_lo, 1)
                pe.wait_ge(o_lo, c + 1)
                for t in range(CT):
                    j = c % GC * CT + t
                    n = 0
                    for k in range(KD):
                        for part in (xo_hi, xo_lo):
                            last = mm(route_ps[g][:, j * 2 * E:(j + 1) * 2 * E],
                                      part[:, c, k, t * P:(t + 1) * P],
                                      gate_hl[:, k, :, :].rearrange("p e s -> p (e s)"),
                                      start=(n == 0), stop=(n == 2 * KD - 1))
                            n += 1
                last.then_inc(logits_done, 1)

            def rows(first, end):
                for n in range(first, end):
                    pe.wait_ge(o_bottom, 2 * n // CT + 1)
                    pe.wait_ge(o_top, 2 * n // CT + 1)
                    if n < 2:
                        pe.wait_ge(cw_lo, n + 1)
                    else:
                        pe.wait_ge(rows_copied, n - 1)
                    for t in range(2):
                        c, tt = (2 * n + t) // CT, (2 * n + t) % CT
                        for k in range(KD):
                            last = nc.tensor.transpose(pair_ps[n % 2][:, t * D + k * P:t * D + (k + 1) * P],
                                                       xo[:, c, k, tt * P:(tt + 1) * P], ident)
                    last.then_inc(rows_done, 1)

            def counts(g):
                pe.wait_ge(mask_ready, g + 1)
                cnt = route_ps[g][:, 0:GJ * E]
                flat = mask16[:, g, :, :].rearrange("p j e -> p (j e)")
                mm(cnt, tri, flat, start=True, stop=False)
                for j in range(GJ - 1):
                    later = GJ - 1 - j
                    mm(route_ps[g][:, (j + 1) * E:GJ * E].rearrange("p (j e) -> p j e", e=E), ones,
                       mask16[:, g, j:j + 1, :].to_broadcast([P, later, E]),
                       start=False, stop=(j == GJ - 2))
                mm(route_ps[g][:, GJ * E:(GJ + 1) * E], ones, msum16[:, g, :],
                   start=True, stop=True).then_inc(counts_done, 1)

            def tokens(g):
                for n in range(2 * GJ):
                    pe.wait_ge(onehot_ready, g * (2 * GJ + 1) + n + 2)
                    last = mm(route_ps[g][:, 0:GT], oh_lane[:, n, :], oh_token[:, n, :],
                              start=(n == 0), stop=(n == 2 * GJ - 1))
                last.then_inc(token_done, 1)

            def w_part(e, part, layer, k, m=None):
                lo = layer * KD * H + k * D
                return w_hl[:, e, part, lo:lo + D] if m is None else w_hl[:, e, part, lo + m * P:lo + (m + 1) * P]

            def shared_first(c, halves=range(KD)):
                if c == 0:
                    pe.wait_ge(w_hi, 1)
                    wait_w_lo(pe, 0)
                pe.wait_ge(o_lo, c + 1)
                for m in halves:
                    n = KD * c + m
                    if c == 0:
                        pe.wait_ge([o_bottom, o_top][m], GC + 1)
                    elif c == 1:
                        pe.wait_ge(rows_copied, G * GJ // 2)
                    elif c == 2:
                        pe.wait_ge(xs_lo, NT)
                        pe.wait_ge(squared, KD * GAP + NQ)
                    else:
                        pe.wait_ge(squared, n - 3 + NQ)
                    terms = [((w_part(E, 0, 0, k, m), w_part(E, 1, 0, k, m)),
                              (xo_hi[:, c, k, :], xo_lo[:, c, k, :])) for k in range(KD)]
                    split_product(first_ps(c, m)[:, :], terms).then_inc(sh1_done, 1)

            def shared_second(c, halves=range(2)):
                pe.wait_ge(sh_hi, KD * (c + 1))
                pe.wait_ge(sh_lo, KD * (c + 1))
                for v in halves:
                    n = 2 * c + v
                    if n < 2:
                        pe.wait_ge(o_bottom, NC)
                        pe.wait_ge(o_top, NC)
                    elif n in (2 * GAP, 2 * GAP + 1):
                        pe.wait_ge(ht_lo, NQ)
                        pe.wait_ge(y_copied, NQ)
                    else:
                        pe.wait_ge(acc_ready, n - 1)
                    for t in range(2):
                        at_ = (2 * v + t) * P
                        terms = [((sh_hl(c)[:, 0, k, at_:at_ + P], sh_hl(c)[:, 1, k, at_:at_ + P]),
                                  (w_part(E, 0, 1, k), w_part(E, 1, 1, k))) for k in range(KD)]
                        last = split_product(out_ps[n % 2][:, t * D:(t + 1) * D], terms)
                    last.then_inc(sh2_done, 1)

            for c in range(NC):
                cond(c)
            logits(0)
            logits(1)
            rows(0, 2)
            logits(2)
            counts(0)
            rows(2, 4)
            shared_first(0)
            tokens(0)
            logits(3)
            rows(4, 8)

            def dyn_w(e, part, layer, k):
                lo = layer * KD * H + k * D
                return w_hl[:, bass.ds(e, 1), part, lo:lo + D]

            def transpose_x(r, n_gathered):
                pe.wait_ge(gathered[r], 32 * n_gathered)
                for t in range(2):
                    for k in range(KD):
                        last = nc.tensor.transpose(x_ps[:, (t * KD + k) * P:(t * KD + k + 1) * P],
                                                   xs[:, r, t, k * P:(k + 1) * P], ident)
                last.then_inc(xt_done, 1)

            def first_layer(experts_, q):
                pe.wait_ge(squared, KD * GAP + q)
                for t in range(2):
                    pe.wait_ge(xs_lo, 2 * q + t + 1)
                    terms = [((xs_hl[:, 0, t, k, :], xs_hl[:, 1, t, k, :]),
                              (dyn_w(experts_[t], 0, 0, k), dyn_w(experts_[t], 1, 0, k))) for k in range(KD)]
                    last = split_product(z_ps[:, t * H:(t + 1) * H], terms)
                last.then_inc(z_done, 1)

            def second_layer(experts_, q):
                pe.wait_ge(ht_lo, q + 1)
                if is_first(q):
                    pe.wait_ge(acc_ready, 2)
                else:
                    pe.wait_ge(y_copied, q)
                for t in range(2):
                    terms = [((ht_hl[:, 0, t, k, :], ht_hl[:, 1, t, k, :]),
                              (dyn_w(experts_[t], 0, 1, k), dyn_w(experts_[t], 1, 1, k))) for k in range(KD)]
                    last = split_product(y_ps[:, t * D:(t + 1) * D], terms)
                last.then_inc(yps_done, 1)

            def transpose_h(q):
                if is_first(q):
                    pe.wait_ge(acc_ready, 1)
                pe.wait_ge(squared, KD * GAP + q + 1)
                for t in range(2):
                    for k in range(KD):
                        last = nc.tensor.transpose(ht_ps[:, (t * KD + k) * P:(t * KD + k + 1) * P],
                                                   hid[:, t * H + k * P:t * H + (k + 1) * P], ident)
                last.then_inc(htr_done, 1)

            wait_w_lo(pe, E)
            pe.wait_ge(o_bottom, NC)
            pe.wait_ge(o_top, NC)
            pe.wait_ge(squared, 1)
            transpose_x(0, 1)
            shared_second(0, [0])

            owner_regs = [pe.alloc_register(f"owner{n}") for n in range(2 * HEAD)]

            def load_experts(first, pairs):
                pe.reg_load(owner_regs[0:2 * pairs], owner[0:1, bass.ds(2 * first, 2 * pairs)])

            def expert_values(n):
                return [pe.snap(r, min_val=0, max_val=E - 1) for r in owner_regs[2 * n:2 * n + 2]]

            def tile_pair(q, slot, turn, now, before, ahead=None, load=None):
                first_layer(now, q)
                if not is_last(q):
                    transpose_x((slot + 1) % RING, turn + (slot + 1) // RING + 1)
                if not is_first(q):
                    second_layer(before, q - 1)
                if is_first(q):
                    shared_second(0, [1])
                if load is not None:
                    load_experts(load, TURN + 1)
                coming = None if ahead is None else expert_values(ahead)
                transpose_h(q)
                return coming

            pe.wait_ge(owners_ready, 1)
            load_experts(0, HEAD)
            now, before = expert_values(0), None
            for q in range(HEAD):
                if q == HEAD - 1:
                    pe.wait_ge(owners_ready, G)
                coming = tile_pair(q, q % RING, q // RING, now, before,
                                   ahead=None if q == HEAD - 1 else q + 1,
                                   load=HEAD - 1 if q == HEAD - 1 else None)
                now, before = coming, now
                if q == COUNTS_AT:
                    counts(1)
                if q == TOKENS_AT:
                    tokens(1)
            with pe.Fori(0, LOOPS) as i:
                before, now = expert_values(0), expert_values(1)
                for u in range(TURN):
                    q0 = HEAD + u
                    coming = tile_pair(TURN * i + q0, q0 % RING, TURN // RING * i + q0 // RING, now, before,
                                       ahead=None if u == TURN - 1 else u + 2,
                                       load=TURN * i + q0 if u == TURN - 1 else None)
                    now, before = coming, now
            before, now = expert_values(0), expert_values(1)
            for u, q in enumerate(TAIL):
                coming = tile_pair(q, q % RING, q // RING, now, before, ahead=None if is_last(q) else u + 2)
                now, before = coming, now
            shared_first(GAP, [0])
            second_layer(before, LAST)
            shared_first(GAP, [1])
            for c in range(GAP + 1, NC):
                shared_first(c)
            for c in range(GAP, NC):
                shared_second(c)

        @block.scalar
        def _(act):
            copy = nc.scalar.activation

            def split_x(c):
                act.wait_ge(x_loaded[c], 16)
                copy(xo_hi[:, c, :, :], xo[:, c, :, :], ACT.Copy).then_inc(x_hi, 1)

            def split_w(n):
                e = (n + E) % (E + 1)
                act.wait_ge(stage_loaded[n % STAGE], 16 * (n // STAGE + 1))
                copy(w_hl[:, e, 0, :], stage[n % STAGE], ACT.Copy).then_inc(w_hi, 1)

            def add_bias(c):
                b = c * CH // SEQ
                if c == 0:
                    act.wait_ge(bias_ready, 1)
                act.wait_ge(cond_done, KD * c + 2)
                act.wait_ge([x_lo, x_lo_pool][c >= DVE_X], c + 1 if c < DVE_X else c + 1 - DVE_X)
                copy(xo[:, c, 1, :], cond_ps[(KD * c + 1) % 4][:, :], ACT.Identity,
                     bias=bias[:, 1, b:b + 1]).then_inc(o_top, 1)

            def split_o(c):
                act.wait_ge(o_bottom, c + 1)
                act.wait_ge(o_top, c + 1)
                copy(xo_hi[:, c, :, :], xo[:, c, :, :], ACT.Copy).then_inc(o_hi, 1)

            def copy_rows(n):
                g = 2 * n // GJ
                act.wait_ge(rows_done, n + 1)
                if n >= ORING:
                    act.wait_ge(rows_written[(n - ORING) // (GJ // 2)][n % ORING], 16)
                copy(orow[:, n % ORING, :, :], pair_ps[n % 2][:, :].rearrange("p (t d) -> p t d", d=D),
                     ACT.Copy).then_inc(rows_copied, 1)
                act.wait_ge(rows_copied, n + 1)
                act.dma_start(rows_v[g][n % (GJ // 2)], orow[:, n % ORING, :, :])\
                    .then_inc(rows_written[g][n % ORING], 16)

            def relu_unit(ps, produced, n_produced, n_squared, buf=0):
                act.wait_ge(produced, n_produced)
                if n_squared is not None:
                    act.wait_ge(squared, n_squared)
                copy(relus[buf], ps[:, :], ACT.Relu).then_inc(relu_done, 1)

            def split_shared(c, m, n, buf=0):
                act.wait_ge(squared, n + 1)
                if c == GAP + 1:
                    act.wait_ge(yps_done, NQ)
                elif c >= 1:
                    act.wait_ge(sh2_done, 2 * max(c - 1, GAP))
                copy(sh_hl(c)[:, 0, m, :], hids[buf], ACT.Copy).then_inc(sh_hi, 1)

            act.wait_ge(small_loaded, 32)
            copy(gate_hl[:, :, :, 0], col("gate").rearrange("p (k e) -> p k e", e=E), ACT.Copy).then_inc(gate_hi, 1)
            split_x(0)
            for b in range(BATCH):
                act.wait_ge(param_done, b + 1)
                copy(cw_hl[:, b, 0, :], pair_ps[b][:, :], ACT.Copy).then_inc(cw_hi, 1)
            for c in range(1, NC):
                split_x(c)
            add_bias(0)
            split_w(0)
            split_o(0)
            add_bias(1)
            split_o(1)
            split_w(1)
            add_bias(2)
            split_w(2)
            add_bias(3)
            split_o(2)
            split_w(3)
            split_o(3)
            split_w(4)
            copy_rows(0)
            split_w(5)
            copy_rows(1)
            split_w(6)
            copy_rows(2)
            copy_rows(3)
            split_w(7)
            split_w(8)
            wait_w_lo(act, 6)
            relu_unit(first_ps(0, 0), sh1_done, 1, None, FRONT)
            split_shared(0, 0, 0, FRONT)
            copy_rows(4)
            relu_unit(first_ps(0, 1), sh1_done, 2, 1, FRONT)
            copy_rows(5)
            split_shared(0, 1, 1, FRONT)
            copy_rows(6)

            def split_xs(q):
                act.wait_ge(xt_done, q + 1)
                if not is_first(q):
                    act.wait_ge(z_done, q)
                copy(xs_hl[:, 0, :, :, :].rearrange("p t k n -> p (t k n)"), x_ps[:, :], ACT.Copy).then_inc(xs_hi, 1)

            def split_ht(q):
                act.wait_ge(htr_done, q + 1)
                if not is_first(q):
                    act.wait_ge(yps_done, q)
                copy(ht_hl[:, 0, :, :, :].rearrange("p t k n -> p (t k n)"), ht_ps[:, :], ACT.Copy).then_inc(ht_hi, 1)

            def copy_y(q, slot, turn):
                act.wait_ge(yps_done, q + 1)
                if not isinstance(turn, int) or turn > 0:
                    act.wait_ge(y_written[slot], 16 * turn)
                copy(y_sb[:, slot, :, :].rearrange("p t d -> p (t d)"), y_ps[:, :], ACT.Copy).then_inc(y_copied, 1)

            UNITS = KD * GAP

            def tile_pair(q, slot, turn):
                relu_unit(z_ps, z_done, q + 1, q + UNITS)
                if not is_last(q):
                    split_xs(q + 1)
                if not is_first(q):
                    copy_y(q - 1, (slot - 1) % RING, turn if slot else turn - 1)
                split_ht(q)

            split_xs(0)
            copy_rows(7)
            act.wait_ge(lg_ready, G)
            copy(gate_s[:, :, :], lg[:, :, :, :].rearrange("p g j e -> p g (j e)"),
                 ACT.Sigmoid).then_inc(sigmoid_done, 1)
            for r in range(2):
                act.wait_ge(rows_written[1][r], 16 * (GJ // (2 * ORING)))
            for_pairs(act, tile_pair)

            def weight_rows(g, first, end):
                act.wait_ge(weights_ready, 1)
                for j in range(first, end):
                    act.wait_ge(fin_loaded[g][j], 32)
                    for c in range(2):
                        copy(fin(g, j, c), fin(g, j, c), ACT.Copy, scale=wgt[:, g, c, j:j + 1]).then_inc(weighted, 1)

            weight_rows(0, 0, 1)
            for r in range(2, ORING):
                act.wait_ge(rows_written[1][r], 16 * (GJ // (2 * ORING)))
            for n in range(KD * GAP, KD * NC + 1):
                if n < KD * NC:
                    relu_unit(first_ps(n // KD, n % KD), sh1_done, n + 1,
                              NQ + (n if n < KD * GAP + 2 else n - 1), n % 2)
                if n == KD * GAP:
                    weight_rows(0, 1, 2)
                    copy_y(LAST, LAST % RING, LAST // RING)
                    weight_rows(0, 2, 3)
                else:
                    split_shared((n - 1) // KD, (n - 1) % KD, n - 1 + NQ, (n - 1) % 2)
                if n == KD * GAP + 2:
                    weight_rows(0, 3, CT * GAP)
            weight_rows(0, CT * GAP, GJ)
            weight_rows(1, 0, GJ - 1)

        @block.vector
        def _(dve):
            tt, ts, stt, red = (nc.vector.tensor_tensor, nc.vector.tensor_scalar,
                                nc.vector.scalar_tensor_tensor, nc.vector.tensor_reduce)
            steps = [0]

            def step(ins):
                ins.then_inc(route_step, 1)
                steps[0] += 1
                dve.wait_ge(route_step, steps[0])

            def split_x(c):
                dve.wait_ge(x_hi, c + 1)
                tt(xo_lo[:, c, :, :], xo[:, c, :, :], xo_hi[:, c, :, :].bitcast(F32), ALU.subtract).then_inc(x_lo, 1)

            def add_bias(c):
                b = c * CH // SEQ
                if c >= DVE_X:
                    dve.wait_ge(x_lo_pool, c + 1 - DVE_X)
                dve.wait_ge(cond_done, KD * c + 1)
                ts(xo[:, c, 0, :], cond_ps[KD * c % 4][:, :], bias[:, 0, b:b + 1], None, ALU.add).then_inc(o_bottom, 1)

            def split_o(c):
                dve.wait_ge(o_hi, c + 1)
                tt(xo_lo[:, c, :, :], xo[:, c, :, :], xo_hi[:, c, :, :].bitcast(F32), ALU.subtract).then_inc(o_lo, 1)

            def choose_one(g, c):
                step(red(best[:, c, :], biased[:, c, :, :], X_AXIS, ALU.max))
                step(tt(score[:, :, :], biased[:, c, :, :],
                        best[:, c, :].unsqueeze(2).to_broadcast([P, GJ, E]), ALU.is_equal))
                step(tt(score[:, :, :], score[:, :, :],
                        col("rank_score").unsqueeze(1).to_broadcast([P, GJ, E]), ALU.mult))
                step(red(top_score[:, :], score[:, :, :], X_AXIS, ALU.max))
                step(tt(sel[:, g, c, :, :], score[:, :, :],
                        top_score[:, :].unsqueeze(2).to_broadcast([P, GJ, E]), ALU.is_equal))

            def choose_best(g):
                dve.wait_ge(logits_done, GC * (g + 1))
                red(lg[:, g, :, :], route_ps[g][:, 0:GJ * 2 * E].rearrange("p (j e s) -> p j e s", e=E, s=2),
                    X_AXIS, ALU.add).then_inc(lg_ready, 1)
                dve.wait_ge(lg_ready, g + 1)
                step(tt(biased[:, 0, :, :], lg[:, g, :, :],
                        col("lb").unsqueeze(1).to_broadcast([P, GJ, E]), ALU.add))
                choose_one(g, 0)

            def choose_second(g):
                step(stt(biased[:, 1, :, :], sel[:, g, 0, :, :], -BIG, biased[:, 0, :, :], ALU.mult, ALU.add))
                choose_one(g, 1)
                step(tt(mask16[:, g, :, :], sel[:, g, 0, :, :], sel[:, g, 1, :, :], ALU.add))
                with nc.allow_low_precision(reason="sums of at most 8 ones are exact in float16"):
                    red(msum16[:, g, :], mask16[:, g, :, :].rearrange("p j e -> p e j"), X_AXIS,
                        ALU.add).then_inc(mask_ready, 1)

            def count_tiles(g):
                dve.wait_ge(counts_done, g + 1)
                step(ts(ntile_i[:, :], route_ps[g][:, GJ * E:(GJ + 1) * E], 1.0 / P,
                        (P - 1) / P - (P - 1) / (2 * P), ALU.mult, ALU.add))
                step(nc.vector.tensor_copy(scan[:, 0, 4:], ntile_i[:, :]))

            def place_experts():
                for n, d in enumerate((1, 2, 4)):
                    step(tt(scan[:, n + 1, 4:], scan[:, n, 4:], scan[:, n, 4 - d:4 + E - d], ALU.add))
                ends = scan[:, 3, 4:]
                step(tt(scan[:, 1, 4:], ends, scan[:, 0, 4:], ALU.subtract))

            def place_slots(g):
                step(stt(slot_e[:, :, :], scan[:, 1, 4:].unsqueeze(1).to_broadcast([P, GJ, E]), float(P),
                         route_ps[g][:, 0:GJ * E].rearrange("p (j e) -> p j e", e=E), ALU.mult, ALU.add))
                step(tt(picked[:, :, :, :].rearrange("p c j e -> p c (j e)"),
                        sel[:, g, :, :, :].rearrange("p c j e -> p c (j e)"),
                        slot_e[:, :, :].rearrange("p j e -> p (j e)").unsqueeze(1).to_broadcast([P, 2, GJ * E]),
                        ALU.mult))
                step(red(slot[:, :, :], picked[:, :, :, :], X_AXIS, ALU.add))

            def place_lanes():
                step(ts(tile_i[:, :, :], slot[:, :, :], 1.0 / P, -(P - 1) / (2 * P), ALU.mult, ALU.add))
                step(nc.vector.tensor_copy(tile_f[:, :, :], tile_i[:, :, :]))
                step(stt(lane_f[:, :, :], tile_f[:, :, :], -float(P), slot[:, :, :], ALU.mult, ALU.add))

            def one_hot_tiles(g):
                if g:
                    dve.wait_ge(token_done, g)
                step(tt(oh_tile[:, :, :], iota_tile.unsqueeze(1).to_broadcast([P, 2 * GJ, GT]),
                        tile_f[:, :, :].rearrange("p c j -> p (c j)").unsqueeze(2).to_broadcast([P, 2 * GJ, GT]),
                        ALU.is_equal))
                token = col("token")
                tt(oh_token[:, :, :].rearrange("p (c j) n -> p c j n", c=2),
                   oh_tile[:, :, :].rearrange("p (c j) n -> p c j n", c=2),
                   token.unsqueeze(1).unsqueeze(3).to_broadcast([P, 2, GJ, GT]), ALU.mult).then_inc(onehot_ready, 1)

            def one_hot_lanes(first, end):
                for n in range(first, end):
                    ts(oh_lane[:, n, :], iota_lane, lane_f[:, n // GJ, n % GJ:n % GJ + 1], None,
                       ALU.is_equal).then_inc(onehot_ready, 1)

            def owners(g):
                step(tt(owner_cmp[:, :, :],
                        pack[0:1, COL["tile_no"][0]:COL["tile_no"][1]].unsqueeze(2).to_broadcast([1, GT, E]),
                        scan[0:1, 3, 4:].unsqueeze(1).to_broadcast([1, GT, E]), ALU.is_ge))
                step(red(owner_f[:, :], owner_cmp[:, :, :], X_AXIS, ALU.add))
                ts(owner[:, g * GT:(g + 1) * GT], owner_f[:, :], float(E - 1), None, ALU.min).then_inc(owners_ready, 1)
                step(ts(slot_i[:, g, :, :], slot[:, :, :], float(g * P), None, ALU.add))

            def token_ids(g):
                dve.wait_ge(token_done, g + 1)
                nc.vector.tensor_copy(token_of[:, g * GT:(g + 1) * GT], route_ps[g][:, 0:GT]).then_inc(token_ready, 1)

            def chosen_gates():
                dve.wait_ge(sigmoid_done, 1)
                for g in range(G):
                    step(tt(gate_of[:, g, :, :, :].rearrange("p c j e -> p c (j e)"),
                            sel[:, g, :, :, :].rearrange("p c j e -> p c (j e)"),
                            gate_s[:, g, :].unsqueeze(1).to_broadcast([P, 2, GJ * E]), ALU.mult))
                step(red(wgt[:, :, :, :], gate_of[:, :, :, :, :], X_AXIS, ALU.add))

            def weights():
                step(tt(wsum[:, :, :], wgt[:, :, 0, :], wgt[:, :, 1, :], ALU.add))
                step(ts(wsum[:, :, :], wsum[:, :, :], 1e-6, None, ALU.add))
                step(nc.vector.reciprocal(wsum[:, :, :], wsum[:, :, :]))
                tt(wgt[:, :, :, :], wgt[:, :, :, :], wsum[:, :, :].unsqueeze(2).to_broadcast([P, G, 2, GJ]),
                   ALU.mult).then_inc(weights_ready, 1)

            def square(ps, n, n_free, free, buf=0):
                dve.wait_ge(relu_done, n + 1)
                if free is not None:
                    dve.wait_ge(free, n_free)
                stt(hids[buf], ps[:, :], 0.0, relus[buf], ALU.max, ALU.mult).then_inc(squared, 1)

            def split_shared(n, buf=0):
                dve.wait_ge(sh_hi, n + 1)
                pair = sh_hl(n // KD)
                tt(pair[:, 1, n % KD, :], hids[buf], pair[:, 0, n % KD, :].bitcast(F32), ALU.subtract)\
                    .then_inc(sh_lo, 1)

            def split_w(n):
                dve.wait_ge(w_hi, n + 1)
                tt(w_hl[:, n - 1, 1, :], stage[n % STAGE], w_hl[:, n - 1, 0, :].bitcast(F32), ALU.subtract)\
                    .then_inc(w_lo_dve, 1)

            def add_shared(n):
                dve.wait_ge(xrows_loaded[n >= 2 * GAP], 16)
                dve.wait_ge(sh2_done, n + 1)
                tt(acc[:, 2 * n:2 * n + 2, :], out_ps[n % 2][:, :].rearrange("p (t d) -> p t d", d=D),
                   acc[:, 2 * n:2 * n + 2, :], ALU.add).then_inc(acc_ready, 1)

            dve.wait_ge(small_loaded, 32)
            step(nc.vector.memset(scan[:, :, :], 0.0))
            step(nc.vector.memset(owner[:, NT:], 0))
            dve.wait_ge(gate_hi, 1)
            tt(gate_hl[:, :, :, 1], col("gate").rearrange("p (k e) -> p k e", e=E),
               gate_hl[:, :, :, 0].bitcast(F32), ALU.subtract).then_inc(gate_lo, 1)
            dve.wait_ge(decoded, WG)
            tt(ut_sb[:, :], route_ps[0][:, 0:D + 1], col("b_dec"), ALU.add).then_inc(ut_ready, 1)
            split_x(0)
            for b in range(BATCH):
                dve.wait_ge(cw_hi, b + 1)
                tt(cw_hl[:, b, 1, :], pair_ps[b][:, :], cw_hl[:, b, 0, :].bitcast(F32), ALU.subtract)\
                    .then_inc(cw_lo, 1)
            dve.wait_ge(param_done, BATCH + 1)
            nc.vector.tensor_copy(bias[:, :, :], cond_ps[3][:, 0:KD * BATCH].rearrange("p (m b) -> p m b", b=BATCH))\
                .then_inc(bias_ready, 1)
            dve.wait_ge(bias_ready, 1)
            split_x(1)
            split_x(2)
            add_bias(0)
            add_bias(1)
            split_o(0)
            split_o(1)
            add_bias(2)
            add_bias(3)
            split_w(DVE_W[0])
            split_o(2)
            choose_best(0)
            choose_second(0)
            split_o(3)
            count_tiles(0)
            place_experts()
            place_slots(0)
            place_lanes()
            one_hot_tiles(0)
            one_hot_lanes(0, 2 * GJ)
            token_ids(0)
            split_w(DVE_W[1])
            UNITS = KD * GAP
            square(first_ps(0, 0), 0, 0, None, FRONT)
            choose_best(1)
            split_shared(0, FRONT)
            square(first_ps(0, 1), 1, 1, sh_lo, FRONT)
            split_shared(1, FRONT)
            owners(0)

            def route_beside(q, place):
                if place == 0:
                    if q == 0:
                        add_shared(1)
                    if q == 1:
                        count_tiles(1)
                    if q == 2:
                        place_slots(1)
                    if q == 3:
                        one_hot_tiles(1)
                    if q >= 4:
                        one_hot_lanes(5 * (q - 4), min(5 * (q - 4) + 2, 2 * GJ))
                if place == 1:
                    if q == 0:
                        chosen_gates()
                    if q == 1:
                        place_experts()
                    if q == 2:
                        place_lanes()
                    if q == 3:
                        owners(1)
                    if 4 <= q < HEAD - 1:
                        one_hot_lanes(5 * (q - 4) + 2, 5 * (q - 3))
                    if q == HEAD - 1:
                        token_ids(1)
                        weights()

            def split_xs(q):
                dve.wait_ge(xs_hi, q)
                for t in range(2):
                    tt(xs_hl[:, 1, t, :, :].rearrange("p k n -> p (k n)"), x_ps[:, t * KD * P:(t + 1) * KD * P],
                       xs_hl[:, 0, t, :, :].rearrange("p k n -> p (k n)").bitcast(F32), ALU.subtract)\
                        .then_inc(xs_lo, 1)

            def split_ht(q):
                dve.wait_ge(ht_hi, q)
                tt(ht_hl[:, 1, :, :, :].rearrange("p t k n -> p (t k n)"), ht_ps[:, :],
                   ht_hl[:, 0, :, :, :].rearrange("p t k n -> p (t k n)").bitcast(F32), ALU.subtract)\
                    .then_inc(ht_lo, 1)

            def tile_pair(q, slot, turn):
                if is_first(q):
                    square(z_ps, UNITS, UNITS, sh_lo)
                else:
                    square(z_ps, q + UNITS, q, htr_done)
                if not is_last(q):
                    split_xs(q + 2)
                if isinstance(q, int) and q < HEAD:
                    route_beside(q, 0)
                split_ht(q + 1)
                if isinstance(q, int) and q < HEAD:
                    route_beside(q, 1)

            split_xs(1)
            choose_second(1)
            add_shared(0)
            for_pairs(dve, tile_pair)

            def combine(g, j, n=1):
                t0 = g * GJ + j
                dve.wait_ge(acc_ready, (t0 + n - 1) // 2 + 1)
                dve.wait_ge(weighted, 2 * (t0 + n))
                first, second = fins(g, j, n, 0), fins(g, j, n, 1)
                tt(first, first, acc[:, t0:t0 + n, :], ALU.add).then_inc(half_ready, n)
                dve.wait_ge(half_ready, t0 + n)
                tt(second, second, first, ALU.add).then_inc(out_ready, n)

            for n in range(KD * GAP, KD * NC + 1):
                if n < KD * NC:
                    free, n_free = (sh_lo, n - 1) if n >= KD * GAP + 2 else (htr_done, NQ)
                    square(first_ps(n // KD, n % KD), n + NQ, n_free, free, n % 2)
                if n > KD * GAP:
                    split_shared(n - 1, (n - 1) % 2)
                if n == KD * GAP:
                    combine(0, 0, 2)
                if n == KD * GAP + 3:
                    combine(0, 2, 2)
                if n == KD * (GAP + 2):
                    add_shared(2 * GAP)
                    add_shared(2 * GAP + 1)
            for c in range(GAP + 1, NC):
                add_shared(2 * c)
                add_shared(2 * c + 1)
                if c == GAP + 1:
                    for j in range(GAP * CT, GJ, 2):
                        combine(0, j, 2)
                    for j in range(0, GJ // 2, 2):
                        combine(1, j, 2)
            combine(1, GJ // 2, 2)
            combine(1, GJ - 2)
            dve.wait_ge(weights_ready, 1)
            dve.wait_ge(fin_loaded[1][GJ - 1], 32)
            last = [fin(1, GJ - 1, c) for c in range(2)]
            w_last = [wgt[:, 1, c, GJ - 1:GJ] for c in range(2)]
            stt(last[0], last[0], w_last[0], acc[:, N // P - 1, :], ALU.mult, ALU.add).then_inc(half_ready, 1)
            dve.wait_ge(half_ready, N // P)
            stt(last[1], last[1], w_last[1], last[0], ALU.mult, ALU.add).then_inc(out_ready, 1)


def kernel(x, cond_512, L0_cond_W_dec, L0_cond_b_dec, L0_cond_V, L0_ffn_gate_w, L0_ffn_lb_bias,
           L0_ffn_w1, L0_ffn_w2, L0_ffn_cfc, L0_ffn_cproj):
    import numpy as np
    import concourse.bacc as bacc
    from concourse.bass_utils import run_bass_kernel_spmd

    def arr(a):
        return np.asarray(a)

    rows = arr(x).reshape(N, D)
    x_t = np.ascontiguousarray(rows.T.reshape(KD, P, NC, CH).transpose(2, 1, 0, 3))
    wdec = np.ascontiguousarray(arr(L0_cond_W_dec).reshape(MU, D + 1, RANK).transpose(0, 2, 1)).reshape(MU, -1)
    b_dec = arr(L0_cond_b_dec).reshape(D + 1, RANK)

    mu = np.zeros((P, BATCH, MUZ), np.float32)
    mu[:, :, LANE - 1] = arr(cond_512).T
    mu = mu.reshape(P, -1)
    small = np.zeros((P, PACK), np.float32)

    def put(name, a):
        small[0:a.shape[0], COL[name][0]:COL[name][1]] = a

    for k in range(RANK):
        for b in range(BATCH):
            row = (k % 2 * BATCH + b) * LANE + k
            small[row, COL["b_dec"][0]:COL["b_dec"][1]] = b_dec[:, k]
            small[row, COL["V"][0] + b * D:COL["V"][0] + (b + 1) * D] = arr(L0_cond_V)[k]
    put("gate", arr(L0_ffn_gate_w).T.reshape(KD, P, E).transpose(1, 0, 2).reshape(P, -1))
    put("lb", np.tile(arr(L0_ffn_lb_bias), (P, 1)))
    put("rank_score", np.tile(np.arange(E, 0, -1, dtype=np.float32), (P, 1)))
    put("token", (np.arange(GJ)[None, :] * P + np.arange(P)[:, None]).astype(np.float32))
    put("tile_no", np.tile(np.arange(GT, dtype=np.float32), (P, 1)))
    put("ident", np.eye(P, dtype=np.float32))
    small16 = np.zeros((P, F16_PACK), np.float16)
    small16[:, F16_TRI:F16_TRI + P] = np.triu(np.ones((P, P), np.float16), 1)
    small16[:, F16_ONES:F16_ONES + P] = 1
    small16[:, F16_IOTA:F16_IOTA + P] = np.arange(P)
    small16[:, F16_TILE:F16_TILE + GT] = np.arange(GT)

    def halves(w):
        return w.T.reshape(KD, P, -1).transpose(1, 0, 2).reshape(P, -1)

    first = [arr(L0_ffn_w1)[e] for e in range(E)] + [arr(L0_ffn_cfc)]
    second = [arr(L0_ffn_w2)[e] for e in range(E)] + [arr(L0_ffn_cproj)]
    experts = np.stack([np.concatenate([halves(a), halves(b)], axis=1) for a, b in zip(first, second)])

    arrays = {"mu_dram": mu, "small_dram": small, "small16_dram": small16, "wdec_dram": wdec, "xT_dram": x_t,
              "xrows_dram": np.ascontiguousarray(rows), "experts_dram": np.ascontiguousarray(experts)}
    nc = bacc.Bacc("TRN2", target_bir_lowering=False, num_devices=1)
    args = [nc.dram_tensor(k, a.shape, mybir.dt.from_np(a.dtype), kind="ExternalInput").ap()
            for k, a in arrays.items()]
    out = nc.dram_tensor("out_dram", (N, D), F32, kind="ExternalOutput").ap()
    build_moe(nc, *args, out)
    r = run_bass_kernel_spmd(nc, [arrays], core_ids=[0])
    return r.results[0]["out_dram"].reshape(BATCH, SEQ, D)
```
